# Optimizing a Trainium2 kernel written in Bass

```python
import numpy as np
import jax
import jax.numpy as jnp

def _softmax(x, axis=-1):
    return jax.nn.softmax(x, axis=axis)

def _gelu(x):
    return jax.nn.gelu(x, approximate=True)

def _silu(x):
    return jax.nn.silu(x)

def _sigmoid(x):
    return jax.nn.sigmoid(x)

def _layernorm(x, axis=-1, eps=1e-05):
    m = jnp.mean(x, axis=axis, keepdims=True)
    v = jnp.var(x, axis=axis, keepdims=True)
    return (x - m) / jnp.sqrt(v + eps)

def _scatter_add(tgt, idx, src, axis=0):
    return tgt.at[idx].add(src)

def _segment_sum(src, seg, n):
    return jax.ops.segment_sum(src, seg, n)
kernel_name = 'mk_adj_resnorm_d1_adj_r2_b04e58'

def setup_inputs(seed: int=0):
    np.random.seed(seed)
    _w = jnp.asarray

    def _rec_inputs():
        import jax
        import jax.numpy as jnp
        _gk = jax.random.key(seed)
        x = -0.0005207 + 1.001 * jax.random.normal(jax.random.fold_in(_gk, 1), (4096, 128), jnp.float32)
        _a = jax.random.bernoulli(jax.random.fold_in(_gk, 2), 0.000976562, (4096, 4096))
        _a = jnp.logical_or(_a, jnp.swapaxes(_a, -1, -2))
        _a = jnp.logical_or(_a, jnp.eye(4096, dtype=bool))
        adj = _a.astype(jnp.int32)
        return (x, adj)
    x, adj = _rec_inputs()

    def _L0_gnn_setup():
        import jax, jax.numpy as jnp
        import numpy as np
        SIZE_U = 2048
        SIZE_V = 2048
        N = SIZE_U + SIZE_V
        D_IN = 128
        QK_DIM = 128
        V_DIM = 128
        HEADS = 2
        DH = QK_DIM // HEADS
        DV = V_DIM // HEADS
        SCALE = DH ** (-0.5)
        NEG_INF = -9000000000000000.0
        key = jax.random.key(seed)
        ks = jax.random.split(key, 8)
        s = 1.0 / np.sqrt(D_IN)
        x = jax.random.normal(ks[0], (N, D_IN), jnp.float32)
        adj = jax.random.randint(ks[1], (N, N), 0, 2, jnp.int32)
        Wq = jax.random.normal(ks[2], (D_IN, QK_DIM), jnp.float32) * s
        Wk = jax.random.normal(ks[3], (D_IN, QK_DIM), jnp.float32) * s
        Wv = jax.random.normal(ks[4], (D_IN, V_DIM), jnp.float32) * s
        weightr = jax.random.normal(ks[5], (V_DIM, V_DIM), jnp.float32) * s
        weightd = jax.random.normal(ks[6], (V_DIM, V_DIM), jnp.float32) * s
        bias = jnp.zeros((V_DIM,), jnp.float32)
        return {'x': x, 'adj': adj, 'Wq': Wq, 'Wk': Wk, 'Wv': Wv, 'weightr': weightr, 'weightd': weightd, 'bias': bias}
    _L0_gnn_all = _L0_gnn_setup()
    _L0_gnn_in = {k: v for k, v in _L0_gnn_all.items() if k in ('Wq', 'Wk', 'Wv', 'weightr', 'weightd', 'bias')}
    del _L0_gnn_all
    return {'x': x, 'adj': adj, 'L0_gnn_Wq': _L0_gnn_in['Wq'], 'L0_gnn_Wk': _L0_gnn_in['Wk'], 'L0_gnn_Wv': _L0_gnn_in['Wv'], 'L0_gnn_weightr': _L0_gnn_in['weightr'], 'L0_gnn_weightd': _L0_gnn_in['weightd'], 'L0_gnn_bias': _L0_gnn_in['bias']}

def reference(x, adj, L0_gnn_Wq, L0_gnn_Wk, L0_gnn_Wv, L0_gnn_weightr, L0_gnn_weightd, L0_gnn_bias):
    import jax
    import jax.numpy as jnp

    def _L0_gnn_ref(x, adj, Wq, Wk, Wv, weightr, weightd, bias):
        import jax, jax.numpy as jnp
        import numpy as np
        SIZE_U = 2048
        SIZE_V = 2048
        N = SIZE_U + SIZE_V
        D_IN = 128
        QK_DIM = 128
        V_DIM = 128
        HEADS = 2
        DH = QK_DIM // HEADS
        DV = V_DIM // HEADS
        SCALE = DH ** (-0.5)
        NEG_INF = -9000000000000000.0
        q = (x @ Wq).reshape(N, HEADS, DH)
        k = (x @ Wk).reshape(N, HEADS, DH)
        v = (x @ Wv).reshape(N, HEADS, DV)
        scores = jnp.einsum('nhd,mhd->hnm', q * SCALE, k)
        scores = jnp.where(adj[None, :, :] > 0, scores, NEG_INF)
        attn = jax.nn.softmax(scores, axis=-1)
        sat = jnp.einsum('hnm,mhd->nhd', attn, v).reshape(N, V_DIM)
        out = jnp.concatenate([sat[:SIZE_U] @ weightr, sat[SIZE_U:] @ weightd], axis=0)
        out = out + bias
        return jax.nn.leaky_relu(out, negative_slope=0.01)
    x = _layernorm(x + _L0_gnn_ref(x, adj, L0_gnn_Wq, L0_gnn_Wk, L0_gnn_Wv, L0_gnn_weightr, L0_gnn_weightd, L0_gnn_bias), axis=-1)
    return x

_drawn_inputs = setup_inputs


def setup_inputs(seed=0):
    import zlib

    import numpy as np

    out = dict(_drawn_inputs(seed))
    spreads = {'L0_gnn_bias': (0.0, 0.1)}
    factors = {}
    for name, (base, spread) in spreads.items():
        noise = np.random.default_rng([zlib.crc32(name.encode()), seed]).standard_normal(out[name].shape)
        drawn = base * np.exp(spread * noise) if base else spread * noise
        out[name] = jnp.asarray(drawn.astype(out[name].dtype))
    for name, factor in factors.items():
        out[name] = (out[name] * factor).astype(out[name].dtype)
    return out
```

```python
from contextlib import ExitStack

import concourse.bass as bass
from concourse import mybir

ALU = mybir.AluOpType
ACT = mybir.ActivationFunctionType
AX = mybir.AxisListType
F32 = mybir.dt.float32
F16 = mybir.dt.float16
BF16 = mybir.dt.bfloat16
I32 = mybir.dt.int32

P = 128
CHUNK = 512
BLOCKS = CHUNK // P
HEADS = 2
DH = 64
SCALE = DH ** -0.5
SLOPE = 0.01
EPS = 1e-5
MASKED = -(2.0 ** 100)
LIMIT = 2.0 ** 14
LIFT = 10.0
EXP_PARTS = 4
WARM_BANKS = 6


def gnn_layer(nc, x, adj, wq, wk, wv, weightr, weightd, bias, out):
    N, D = x.shape
    TILES = N // P
    PAIRS = TILES // 2
    CH = N // CHUNK
    PAIR_CHUNKS = 4 * CH
    AHEAD = 2 * CH
    TURN_AHEAD = 3
    PARTW = N // EXP_PARTS
    PART_CHUNKS = CH // EXP_PARTS
    assert D == P and HEADS * DH == P and CH == 8

    x_tiles = x.rearrange("(t p) d -> p t d", p=P)
    adj_tiles = adj.rearrange("(t p) m -> p t m", p=P)
    out_tiles = out.rearrange("(t p) d -> p t d", p=P)
    X_LOADS = 4

    with ExitStack() as ctx:
        def sb(name, shape, dt):
            return ctx.enter_context(nc.sbuf_tensor(name, shape, dt))

        def sem(name):
            return ctx.enter_context(nc.semaphore(name))

        x_rows = sb("x_rows", [P, TILES, P], F32)
        x_cols = sb("x_cols", [P, N], F32)
        w_qk = sb("w_qk", [P, 2, HEADS, 2, DH], F32)
        w_v = sb("w_v", [P, P], F32)
        w_out = sb("w_out", [P, 2, P], F32)
        bias_rows = sb("bias_rows", [P, P], F32)
        ident = sb("ident", [P, P], F32)
        q_split = sb("q_split", [P, HEADS, N], F16)
        k_hi = sb("k_hi", [P, HEADS, N], F16)
        k_lo = sb("k_lo", [P, HEADS, N], F16)
        v_split = sb("v_split", [P, TILES, HEADS, 2, DH], F16)
        adj_in = sb("adj_in", [P, 2, N], I32)
        mask = sb("mask", [P, 2, N], BF16)
        rows = sb("rows", [P, HEADS, N], F32)
        p_hi = sb("p_hi", [P, 4, CHUNK], F16)
        p_lo = sb("p_lo", [P, 4, CHUNK], F16)
        maxes = sb("maxes", [P, HEADS, CH], F32)
        top = sb("top", [P, HEADS], F32)
        shift = sb("shift", [P, HEADS], F32)
        sums = sb("sums", [P, 2, HEADS, EXP_PARTS], F32)
        total = sb("total", [P, 2, HEADS], F32)
        inverse = sb("inverse", [P, 2, HEADS], F32)
        side = sb("side", [P, HEADS, DH], F32)
        sat = sb("sat", [P, HEADS * DH], F32)
        sat_cols = sb("sat_cols", [P, P], F32)
        linear = sb("linear", [P, P], F32)
        active = sb("active", [P, P], F32)
        resid = sb("resid", [P, 2, P], F32)
        stats = sb("stats", [P, 6], F32)
        moments = sb("moments", [P, 2, 2], F32)
        rstd = sb("rstd", [P, 2], F32)
        powers = sb("powers", [P, 2], F32)
        normed = sb("normed", [P, 2, P], F32)
        peaks = sb("peaks", [P, 8], F32)
        peaks_all = sb("peaks_all", [P, 8], F32)
        x_peak = sb("x_peak", [P, 1], F32)
        bounds = sb("bounds", [P, 3], F32)
        pow2 = sb("pow2", [P, 3], F32)
        recip2 = sb("recip2", [P, 3], F32)
        factors = sb("factors", [P, 3], F32)
        qk_pow2 = sb("qk_pow2", [P, 1], F32)
        exp_scale = sb("exp_scale", [P, 1], F32)
        neg_scale = sb("neg_scale", [P, 1], F32)
        v_back = sb("v_back", [P, 1], F32)

        ps = ctx.enter_context(nc.psum_tensor("ps", [P, 8, CHUNK], F32))
        SCORE, TURN, SAT = 0, 2, 6
        SIDE_T, SIDE_P = P, 2 * P

        x_loaded = [sem(f"x_loaded{i}") for i in range(X_LOADS)]
        weights_loaded = sem("weights_loaded")
        ends_loaded = sem("ends_loaded")
        adj_loaded = [sem(f"adj_loaded{i}") for i in range(2)]
        ident_ready = sem("ident_ready")
        powers_ready = sem("powers_ready")
        peaks_ready = sem("peaks_ready")
        peaks_shared = sem("peaks_shared")
        setup = sem("setup")
        x_turned = sem("x_turned")
        x_taken = sem("x_taken")
        projected = sem("projected")
        hi_split = sem("hi_split")
        lo_split = sem("lo_split")
        masked = sem("masked")
        scored = sem("scored")
        scores_taken = sem("scores_taken")
        tops_ready = sem("tops_ready")
        shifts_ready = sem("shifts_ready")
        probs_ready = sem("probs_ready")
        turned = sem("turned")
        hi_ready = sem("hi_ready")
        lo_ready = sem("lo_ready")
        attended = sem("attended")
        totals_ready = sem("totals_ready")
        inverse_ready = sem("inverse_ready")
        side_ready = sem("side_ready")
        merged = sem("merged")
        sat_turned = sem("sat_turned")
        sat_ready = sem("sat_ready")
        sat_projected = sem("sat_projected")
        linear_ready = sem("linear_ready")
        active_ready = sem("active_ready")
        resid_ready = sem("resid_ready")
        stats_ready = sem("stats_ready")
        moments_ready = sem("moments_ready")
        rstd_ready = sem("rstd_ready")
        normed_ready = sem("normed_ready")
        stored = [sem(f"stored{i}") for i in range(2)]

        SETUP_STEPS = 11
        carrier = {name: sem(f"carrier_{name}") for name in ("DVE", "Pool")}

        def wait(eng, s, value):
            if not isinstance(value, int) or value > 0:
                eng.wait_ge(s, value)

        jobs = [("q", 0, 0)] + [("k", 0, c) for c in range(CH)]
        jobs += [("q", 1, 0)] + [("k", 1, c) for c in range(CH)]
        early = len(jobs)
        jobs += [("v", 0, c) for c in range(CH)]
        jobs += [("q", h, c) for c in range(1, CH) for h in range(HEADS)]
        warm = [("job", n) for n in range(early)]
        for i in range(max(len(jobs) - early, AHEAD)):
            if i < len(jobs) - early:
                warm.append(("job", early + i))
            if i < AHEAD:
                warm.append(("score", i))

        def wait_apart(eng, s, value):
            eng.wait_ge(s, value)
            if not isinstance(value, int):
                eng.sem_inc(carrier[eng.engine.name], 1)

        def warm_bank(n):
            return 2 + (n + CH) % WARM_BANKS

        block = ctx.enter_context(nc.Block())

        @block.sync
        def _(sp):
            def load_adj(t, q, par):
                wait(sp, masked, EXP_PARTS * (t - 1) if not isinstance(t, int) or t >= 2 else 0)
                sp.dma_start(adj_in[:, par, :], adj_tiles[:, t, :]).then_inc(adj_loaded[par], 16)

            def store(t, par):
                sp.wait_ge(normed_ready, t + 1)
                sp.dma_start(out_tiles[:, t, :], normed[:, par, :]).then_inc(stored[par], 16)

            for r in range(2):
                sp.dma_start(w_qk[:, 0, :, r, :], wq.rearrange("i (h d) -> i h d", h=HEADS)).then_inc(weights_loaded, 16)
                sp.dma_start(w_qk[:, 1, :, r, :], wk.rearrange("i (h d) -> i h d", h=HEADS)).then_inc(weights_loaded, 16)
            sp.dma_start(w_v[:, :], wv).then_inc(weights_loaded, 16)
            per = TILES // X_LOADS
            for i in range(X_LOADS):
                sp.dma_start(x_rows[:, i * per:(i + 1) * per, :], x_tiles[:, i * per:(i + 1) * per, :])\
                  .then_inc(x_loaded[i], 16)
            sp.dma_start(w_out[:, 0, :], weightr).then_inc(ends_loaded, 16)
            sp.dma_start(w_out[:, 1, :], weightd).then_inc(ends_loaded, 16)
            sp.dma_start(bias_rows[:, :], bias.partition_broadcast(P)).then_inc(ends_loaded, 16)

            LAG = 5
            for t in range(6):
                load_adj(t, t // 2, t % 2)
                if t >= LAG:
                    store(t - LAG, (t - LAG) % 2)
            with sp.Fori(3, PAIRS) as q:
                for r in range(2):
                    load_adj(2 * q + r, q, r)
                    store(2 * q + r - LAG, (r - LAG) % 2)
            for t in range(TILES - LAG, TILES):
                store(t, t % 2)
            sp.wait_ge(stored[0], 16 * PAIRS)
            sp.wait_ge(stored[1], 16 * PAIRS)

        @block.gpsimd
        def _(pool):
            nc.gpsimd.memset(ident[:, :], 0.0).then_inc(ident_ready, 1)
            pool.wait_ge(ident_ready, 1)
            nc.gpsimd.affine_select(out=ident[:, :], in_=ident[:, :], compare_op=ALU.not_equal, fill=1.0,
                                    base=0, pattern=[[-1, P]], channel_multiplier=1).then_inc(ident_ready, 1)
            nc.gpsimd.memset(powers[:, 0:1], EPS).then_inc(powers_ready, 1)
            nc.gpsimd.memset(powers[:, 1:2], -0.5).then_inc(powers_ready, 1)
            pool.wait_ge(peaks_ready, X_LOADS + 4)
            nc.gpsimd.partition_all_reduce(peaks_all[:, :], peaks[:, :], P, bass.bass_isa.ReduceOp.max)\
              .then_inc(peaks_shared, 1)

            def make_mask(t, q, par, part):
                if part == 0:
                    if not isinstance(t, int) or t >= 2:
                        wait_apart(pool, scores_taken, 2 * CH * (t - 1))
                    wait_apart(pool, adj_loaded[par], 16 * (q + 1))
                c = slice(part * PARTW, (part + 1) * PARTW)
                nc.gpsimd.tensor_scalar(mask[:, par, c], adj_in[:, par, c], 0.0, MASKED, ALU.is_le, ALU.mult)\
                  .then_inc(masked, 1)

            def inverse_deviation(t, par):
                pool.wait_ge(moments_ready, t + 1)
                nc.gpsimd.tensor_tensor(rstd[:, par:par + 1], moments[:, par, 1:2], powers[:, 1:2], ALU.pow)\
                  .then_inc(rstd_ready, 1)

            def mask_pair(q, first):
                for r in range(2):
                    for part in range(EXP_PARTS):
                        make_mask(2 * q + r, q, r, part)
                        if part == 2 and not (first and 2 * q + r < 3):
                            inverse_deviation(2 * q + r - 3, (r - 3) % 2)

            pool.wait_ge(powers_ready, 2)
            mask_pair(0, True)
            mask_pair(1, True)
            with pool.Fori(2, PAIRS) as q:
                mask_pair(q, False)
            for t in range(TILES - 3, TILES):
                inverse_deviation(t, t % 2)

        @block.scalar
        def _(act):
            def exps(unit, h, tile_par, part):
                if part == 0:
                    act.wait_ge(shifts_ready, unit + 1)
                c = slice(part * PARTW, (part + 1) * PARTW)
                nc.scalar.activation(rows[:, h, c], rows[:, h, c], ACT.Exp, bias=shift[:, h:h + 1],
                                     scale=exp_scale[:, :], accum_out=sums[:, tile_par, h, part:part + 1])\
                  .then_inc(probs_ready, 1)

            def upper_part(g, slot):
                act.wait_ge(turned, g + 1)
                wait(act, attended, g - 3)
                nc.scalar.copy(p_hi[:, slot, :], ps[:, TURN + slot, :]).then_inc(hi_ready, 1)

            def side_of(unit, h, tile, par):
                act.wait_ge(attended, CH * (unit + 1))
                act.wait_ge(inverse_ready, tile + 1)
                nc.scalar.mul(side[:, h, :], ps[:, SAT + h, DH:2 * DH], inverse[:, par, h:h + 1]).then_inc(side_ready, 1)

            def sat_copy(tile):
                act.wait_ge(sat_turned, tile + 1)
                nc.scalar.copy(sat_cols[:, :], ps[:, SAT + 1, SIDE_T:SIDE_T + P]).then_inc(sat_ready, 1)

            for n in range(CH):
                act.wait_ge(x_turned, n + 1)
                nc.scalar.copy(x_cols[:, n * CHUNK:(n + 1) * CHUNK], ps[:, 2 + n % WARM_BANKS, :]).then_inc(x_taken, 1)
            act.wait_ge(setup, SETUP_STEPS)
            exp_at = {CH + 1 + 2 * k: k for k in range(EXP_PARTS)}
            for kind, n in warm:
                if kind == "job":
                    what, h, c = jobs[n]
                    act.wait_ge(projected, n + 1)
                    src = ps[:, warm_bank(n), :]
                    cols = slice(c * CHUNK, (c + 1) * CHUNK)
                    if what == "q":
                        nc.scalar.mul(q_split[:, h, cols], src, factors[:, 0:1]).then_inc(hi_split, 1)
                    elif what == "k":
                        nc.scalar.mul(k_hi[:, h, cols], src, factors[:, 1:2]).then_inc(hi_split, 1)
                    else:
                        dst = v_split[:, c * BLOCKS:(c + 1) * BLOCKS, :, 0, :].rearrange("p t h d -> p (t h) d")
                        nc.scalar.mul(dst, src.rearrange("p (a d) -> p a d", d=DH), factors[:, 2:3]).then_inc(hi_split, 1)
                elif n in exp_at:
                    exps(0, 0, 0, exp_at[n])
            for l in range(TURN_AHEAD):
                upper_part(l, l)

            def pair(p, first, last):
                for l in range(PAIR_CHUNKS):
                    k, j = divmod(l, CH)
                    h, r = k % 2, k // 2
                    g, unit, tile = p * PAIR_CHUNKS + l, 4 * p + k, 2 * p + r
                    if not (last and l + TURN_AHEAD >= PAIR_CHUNKS):
                        upper_part(g + TURN_AHEAD, (l + TURN_AHEAD) % 4)
                    if j < EXP_PARTS and not (last and k == 3):
                        exps(unit + 1, (h + 1) % 2, ((k + 1) // 2) % 2, j)
                    if h == 1 and j == 1:
                        side_of(unit - 1, 0, tile, r)
                    if h == 0 and not (first and k == 0):
                        if j == 1:
                            side_of(unit - 1, 1, tile - 1, (r - 1) % 2)
                        if j == 3:
                            sat_copy(tile - 1)

            pair(0, True, False)
            with act.Fori(1, PAIRS - 1) as p:
                pair(p, False, False)
            pair(PAIRS - 1, False, True)
            side_of(2 * TILES - 1, 1, TILES - 1, 1)
            sat_copy(TILES - 1)

        @block.vector
        def _(dve):
            def mask_max(g, h, tile, tile_par, j, slot):
                if h == 0 and j % PART_CHUNKS == 0:
                    dve.wait_ge(masked, EXP_PARTS * tile + j // PART_CHUNKS + 1)
                wait(dve, turned, g - AHEAD + 1)
                wait_apart(dve, scored, g + 1)
                c = slice(j * CHUNK, (j + 1) * CHUNK)
                nc.vector.tensor_tensor_reduce(out=rows[:, h, c], in0=ps[:, SCORE + slot, :], in1=mask[:, tile_par, c],
                                               scale=1.0, scalar=2 * MASKED, op0=ALU.add, op1=ALU.max,
                                               accum_out=maxes[:, h, j:j + 1]).then_inc(scores_taken, 1)

            def shift_of(unit, h):
                dve.wait_ge(scores_taken, CH * (unit + 1))
                nc.vector.tensor_reduce(top[:, h:h + 1], maxes[:, h, :], AX.X, ALU.max).then_inc(tops_ready, 1)
                dve.wait_ge(tops_ready, unit + 1)
                nc.vector.tensor_scalar(shift[:, h:h + 1], top[:, h:h + 1], neg_scale[:, :], LIFT, ALU.mult, ALU.add)\
                  .then_inc(shifts_ready, 1)

            def lower_part(g, slot):
                dve.wait_ge(hi_ready, g + 1)
                nc.vector.tensor_tensor(p_lo[:, slot, :], ps[:, TURN + slot, :], p_hi[:, slot, :], ALU.subtract)\
                  .then_inc(lo_ready, 1)

            def invert_sums(unit, tile, par):
                dve.wait_ge(probs_ready, EXP_PARTS * (unit + 1))
                nc.vector.tensor_reduce(total[:, par, :], sums[:, par, :, :], AX.X, ALU.add).then_inc(totals_ready, 1)
                dve.wait_ge(totals_ready, tile + 1)
                nc.vector.reciprocal(inverse[:, par, :], total[:, par, :]).then_inc(inverse_ready, 1)

            def merge(unit, h, tile, par):
                dve.wait_ge(side_ready, unit + 1)
                if h == 0:
                    wait(dve, sat_turned, tile)
                nc.vector.scalar_tensor_tensor(out=sat[:, h * DH:(h + 1) * DH], in0=ps[:, SAT + h, 0:DH],
                                               scalar=inverse[:, par, h:h + 1], in1=side[:, h, :],
                                               op0=ALU.mult, op1=ALU.add).then_inc(merged, 1)

            def add_bias(tile):
                dve.wait_ge(sat_projected, tile + 1)
                nc.vector.tensor_tensor(linear[:, :], ps[:, SAT + 1, SIDE_P:SIDE_P + P], bias_rows[:, :], ALU.add)\
                  .then_inc(linear_ready, 1)

            def leaky(tile):
                dve.wait_ge(linear_ready, tile + 1)
                nc.vector.scalar_tensor_tensor(out=active[:, :], in0=linear[:, :], scalar=SLOPE, in1=linear[:, :],
                                               op0=ALU.mult, op1=ALU.max).then_inc(active_ready, 1)

            def add_x(tile, par):
                dve.wait_ge(active_ready, tile + 1)
                nc.vector.tensor_tensor(resid[:, par, :], active[:, :], x_flat[:, bass.ds(tile * P, P)], ALU.add)\
                  .then_inc(resid_ready, 1)

            def statistics(tile, par):
                wait_apart(dve, resid_ready, tile + 1)
                nc.vector.bn_stats(stats[:, :], resid[:, par, :]).then_inc(stats_ready, 1)

            def mean_variance(tile, par):
                wait_apart(dve, stats_ready, 2 * tile + 1)
                nc.vector.bn_aggr(moments[:, par, :], stats[:, :]).then_inc(stats_ready, 1)
                dve.wait_ge(stats_ready, 2 * tile + 2)
                nc.vector.tensor_scalar(moments[:, par, 1:2], moments[:, par, 1:2], EPS, None, ALU.add)\
                  .then_inc(moments_ready, 1)

            def normalise(tile, pairs_before, par):
                dve.wait_ge(rstd_ready, tile + 1)
                wait(dve, stored[par], 16 * pairs_before)
                nc.vector.tensor_scalar(normed[:, par, :], resid[:, par, :], moments[:, par, 0:1],
                                        rstd[:, par:par + 1], ALU.subtract, ALU.mult).then_inc(normed_ready, 1)

            x_flat = x_rows[:, :, :].rearrange("p t d -> p (t d)")

            nc.vector.memset(peaks[:, 7:8], 0.0).then_inc(peaks_ready, 1)
            dve.wait_ge(weights_loaded, 16 * 5)
            for i in range(2):
                nc.vector.tensor_reduce(peaks[:, 4 + i:5 + i], w_qk[:, i, :, 0, :], AX.XY, ALU.max,
                                        apply_absolute_value=True).then_inc(peaks_ready, 1)
            nc.vector.tensor_reduce(peaks[:, 6:7], w_v[:, :], AX.X, ALU.max, apply_absolute_value=True)\
              .then_inc(peaks_ready, 1)
            per = TILES // X_LOADS * P
            for i in range(X_LOADS):
                dve.wait_ge(x_loaded[i], 16)
                nc.vector.tensor_reduce(peaks[:, i:i + 1], x_flat[:, i * per:(i + 1) * per], AX.X, ALU.max,
                                        apply_absolute_value=True).then_inc(peaks_ready, 1)
            dve.wait_ge(peaks_shared, 1)
            nc.vector.tensor_reduce(x_peak[:, :], peaks_all[:, 0:X_LOADS], AX.X, ALU.max).then_inc(setup, 1)
            dve.wait_ge(setup, 1)
            nc.vector.tensor_scalar(bounds[:, :], peaks_all[:, 4:7], x_peak[:, :], float(D), ALU.mult, ALU.mult)\
              .then_inc(setup, 1)
            dve.wait_ge(setup, 2)
            nc.vector.tensor_scalar(recip2[:, :], bounds[:, :], 2.0 ** -60, None, ALU.max).then_inc(setup, 1)
            dve.wait_ge(setup, 3)
            nc.vector.tensor_scalar(pow2[:, :].bitcast(I32), recip2[:, :].bitcast(I32), 0x7F800000, None,
                                    ALU.bitwise_and).then_inc(setup, 1)
            dve.wait_ge(setup, 4)
            nc.vector.reciprocal(recip2[:, :], pow2[:, :]).then_inc(setup, 1)
            dve.wait_ge(setup, 5)
            nc.vector.tensor_scalar(factors[:, :], recip2[:, :], LIMIT, None, ALU.mult).then_inc(setup, 1)
            nc.vector.tensor_tensor(qk_pow2[:, :], pow2[:, 0:1], pow2[:, 1:2], ALU.mult).then_inc(setup, 1)
            dve.wait_ge(setup, 7)
            nc.vector.tensor_scalar(exp_scale[:, :], qk_pow2[:, :], SCALE / LIMIT ** 2, None, ALU.mult).then_inc(setup, 1)
            nc.vector.tensor_scalar(neg_scale[:, :], qk_pow2[:, :], -SCALE / LIMIT ** 2, None, ALU.mult)\
              .then_inc(setup, 1)
            nc.vector.tensor_scalar(v_back[:, :], pow2[:, 2:3], 1.0 / LIMIT, None, ALU.mult).then_inc(setup, 1)
            dve.wait_ge(setup, 10)
            dve.wait_ge(ends_loaded, 16 * 3)
            nc.vector.tensor_scalar(w_out[:, :, :], w_out[:, :, :], v_back[:, :], None, ALU.mult).then_inc(setup, 1)

            for kind, n in warm:
                if kind == "job":
                    what, h, c = jobs[n]
                    dve.wait_ge(hi_split, n + 1)
                    cols = slice(c * CHUNK, (c + 1) * CHUNK)
                    if what == "q":
                        part = q_split[DH:P, h, cols]
                        nc.vector.scalar_tensor_tensor(out=part, in0=ps[DH:P, warm_bank(n), :], scalar=factors[DH:P, 0:1],
                                                       in1=part, op0=ALU.mult, op1=ALU.subtract).then_inc(lo_split, 1)
                    elif what == "k":
                        nc.vector.scalar_tensor_tensor(out=k_lo[:, h, cols], in0=ps[:, warm_bank(n), :],
                                                       scalar=factors[:, 1:2], in1=k_hi[:, h, cols],
                                                       op0=ALU.mult, op1=ALU.subtract).then_inc(lo_split, 1)
                    else:
                        v = v_split[:, c * BLOCKS:(c + 1) * BLOCKS, :, :, :].rearrange("p t h s d -> p (t h) s d")
                        nc.vector.scalar_tensor_tensor(
                            out=v[:, :, 1, :], in0=ps[:, warm_bank(n), :].rearrange("p (a d) -> p a d", d=DH),
                            scalar=factors[:, 2:3], in1=v[:, :, 0, :], op0=ALU.mult, op1=ALU.subtract)\
                          .then_inc(lo_split, 1)
                else:
                    h, j = divmod(n, CH)
                    mask_max(n, h, 0, 0, j, n % 2)
                    if j == CH - 1:
                        shift_of(h, h)
            for l in range(TURN_AHEAD - 1):
                lower_part(l, l)

            def pair(p, first, last):
                for l in range(PAIR_CHUNKS):
                    k, j = divmod(l, CH)
                    h, r = k % 2, k // 2
                    g, unit, tile = p * PAIR_CHUNKS + l, 4 * p + k, 2 * p + r
                    if not (last and l + TURN_AHEAD - 1 >= PAIR_CHUNKS):
                        lower_part(g + TURN_AHEAD - 1, (l + TURN_AHEAD - 1) % 4)
                    if not (last and k >= 2):
                        mask_max(g + AHEAD, h, tile + 1, (r + 1) % 2, j, l % 2)
                        if j == CH - 1:
                            shift_of(unit + 2, h)
                    if h == 0 and not (first and k == 0):
                        if j == 1:
                            merge(unit - 1, 1, tile - 1, (r - 1) % 2)
                        if j == 5:
                            add_bias(tile - 1)
                        if j == 6:
                            leaky(tile - 1)
                        if j == 7:
                            add_x(tile - 1, (r - 1) % 2)
                    if h == 1:
                        if not (first and k == 1):
                            if j == 0:
                                statistics(tile - 1, (r - 1) % 2)
                            if j == 2:
                                mean_variance(tile - 1, (r - 1) % 2)
                            if j == 7:
                                normalise(tile - 1, (p if r == 1 else p - 1), (r - 1) % 2)
                        if j == 0:
                            invert_sums(unit, tile, r)
                        if j == 1:
                            merge(unit - 1, 0, tile, r)

            pair(0, True, False)
            with dve.Fori(1, PAIRS - 1) as p:
                pair(p, False, False)
            pair(PAIRS - 1, False, True)
            t = TILES - 1
            merge(2 * t + 1, 1, t, 1)
            add_bias(t)
            leaky(t)
            add_x(t, 1)
            statistics(t, 1)
            mean_variance(t, 1)
            normalise(t, PAIRS - 1, 1)

        @block.tensor
        def _(pe):
            def score(g, h, tile, j, slot):
                wait(pe, scores_taken, g - 1)
                lhsT = q_split[:, h, bass.ds(tile * P, P)]
                c = slice(j * CHUNK, (j + 1) * CHUNK)
                nc.tensor.matmul(ps[:, SCORE + slot, :], lhsT, k_hi[:, h, c], start=True, stop=False)
                nc.tensor.matmul(ps[:, SCORE + slot, :], lhsT, k_lo[:, h, c], start=False, stop=True).then_inc(scored, 1)

            def turn(g, unit, h, j, slot):
                if j % PART_CHUNKS == 0:
                    pe.wait_ge(probs_ready, EXP_PARTS * unit + j // PART_CHUNKS + 1)
                wait(pe, lo_ready, g - 3)
                for b in range(BLOCKS):
                    c = slice(j * CHUNK + b * P, j * CHUNK + (b + 1) * P)
                    last = nc.tensor.transpose(ps[:, TURN + slot, b * P:(b + 1) * P], rows[:, h, c], ident[:, :])
                last.then_inc(turned, 1)

            def attend(g, unit, tile, h, j, slot):
                pe.wait_ge(lo_ready, g + 1)
                if j == 0:
                    wait(pe, merged, unit - 1)
                    if h == 1:
                        wait(pe, linear_ready, tile)
                for b in range(BLOCKS):
                    c = slice(b * P, (b + 1) * P)
                    v = v_split[:, j * BLOCKS + b, h, :, :].rearrange("p s d -> p (s d)")
                    nc.tensor.matmul(ps[:, SAT + h, 0:2 * DH], p_hi[:, slot, c], v,
                                     start=(j == 0 and b == 0), stop=False, skip_group_check=True)
                    last = nc.tensor.matmul(ps[:, SAT + h, 0:DH], p_lo[:, slot, c], v[:, 0:DH], start=False,
                                            stop=(j == CH - 1 and b == BLOCKS - 1), skip_group_check=True)
                last.then_inc(attended, 1)

            def turn_sat(tile):
                pe.wait_ge(merged, 2 * tile + 2)
                nc.tensor.transpose(ps[:, SAT + 1, SIDE_T:SIDE_T + P], sat[:, :], ident[:, :]).then_inc(sat_turned, 1)

            def project_sat(tile):
                pe.wait_ge(sat_ready, tile + 1)
                w = w_out[:, :, :].rearrange("p s d -> p (s d)")[:, bass.ds(tile // (TILES // 2) * P, P)]
                nc.tensor.matmul(ps[:, SAT + 1, SIDE_P:SIDE_P + P], sat_cols[:, :], w, start=True, stop=True)\
                  .then_inc(sat_projected, 1)

            pe.wait_ge(ident_ready, 2)
            for n in range(CH):
                if n % 2 == 0:
                    pe.wait_ge(x_loaded[n // 2], 16)
                wait(pe, x_taken, n - WARM_BANKS + 1)
                for b in range(BLOCKS):
                    last = nc.tensor.transpose(ps[:, 2 + n % WARM_BANKS, b * P:(b + 1) * P],
                                               x_rows[:, n * BLOCKS + b, :], ident[:, :])
                last.then_inc(x_turned, 1)
            pe.wait_ge(weights_loaded, 16 * 5)
            for kind, n in warm:
                if kind == "score":
                    h, j = divmod(n, CH)
                    if n == 0:
                        pe.wait_ge(lo_split, early)
                    score(n, h, 0, j, n % 2)
                    continue
                what, h, c = jobs[n]
                if n < WARM_BANKS:
                    pe.wait_ge(x_taken, max(n + CH - WARM_BANKS, c) + 1)
                else:
                    pe.wait_ge(lo_split, n - WARM_BANKS + 1)
                    if n < WARM_BANKS + CH:
                        pe.wait_ge(x_taken, CH)
                bank = warm_bank(n)
                if what == "v":
                    for b in range(BLOCKS):
                        keys = slice(c * CHUNK + b * P, c * CHUNK + (b + 1) * P)
                        last = nc.tensor.matmul(ps[:, bank, b * P:(b + 1) * P], x_cols[:, keys], w_v[:, :],
                                                start=True, stop=True)
                else:
                    w = w_qk[:, 0 if what == "q" else 1, h, :, :].rearrange("p r d -> p (r d)")
                    last = nc.tensor.matmul(ps[:, bank, :], w, x_cols[:, c * CHUNK:(c + 1) * CHUNK], start=True, stop=True)
                last.then_inc(projected, 1)
            pe.wait_ge(lo_split, len(jobs))
            for l in range(TURN_AHEAD):
                turn(l, 0, 0, l, l)

            def pair(p, last):
                for l in range(PAIR_CHUNKS):
                    k, j = divmod(l, CH)
                    h, r = k % 2, k // 2
                    g, unit, tile = p * PAIR_CHUNKS + l, 4 * p + k, 2 * p + r
                    if not (last and l + TURN_AHEAD >= PAIR_CHUNKS):
                        ahead = l + TURN_AHEAD
                        turn(g + TURN_AHEAD, 4 * p + ahead // CH, ahead // CH % 2, ahead % CH, ahead % 4)
                    if not (last and k >= 2):
                        score(g + AHEAD, h, tile + 1, j, l % 2)
                    attend(g, unit, tile, h, j, l % 4)
                    if h == 0 and not (isinstance(p, int) and p == 0 and k == 0):
                        if j == 2:
                            turn_sat(tile - 1)
                        if j == 4:
                            project_sat(tile - 1)

            pair(0, False)
            with pe.Fori(1, PAIRS - 1) as p:
                pair(p, False)
            pair(PAIRS - 1, True)
            turn_sat(TILES - 1)
            pe.wait_ge(setup, SETUP_STEPS)
            project_sat(TILES - 1)


_INS = ["x", "adj", "L0_gnn_Wq", "L0_gnn_Wk", "L0_gnn_Wv", "L0_gnn_weightr", "L0_gnn_weightd", "L0_gnn_bias"]


def kernel(**inputs):
    import numpy as _np
    import concourse.bacc as _bacc
    from concourse import mybir as _mybir
    from concourse.bass_utils import run_bass_kernel_spmd as _run

    nc = _bacc.Bacc("TRN2", target_bir_lowering=False, num_devices=1)
    arrays, args = {}, []
    for name in _INS:
        a = _np.ascontiguousarray(inputs[name])
        arrays[f"in_{name}_dram"] = a
        args.append(nc.dram_tensor(f"in_{name}_dram", a.shape, _mybir.dt.from_np(a.dtype), kind="ExternalInput").ap())
    shape = inputs["x"].shape
    args.append(nc.dram_tensor("out_0_dram", shape, _mybir.dt.float32, kind="ExternalOutput").ap())
    gnn_layer(nc, *args)
    r = _run(nc, [arrays], core_ids=[0])
    return r.results[0]["out_0_dram"]
```

```python
from contextlib import ExitStack

import concourse.bass as bass
from concourse import mybir

ALU = mybir.AluOpType
ACT = mybir.ActivationFunctionType
AX = mybir.AxisListType
F32 = mybir.dt.float32
F16 = mybir.dt.float16
BF16 = mybir.dt.bfloat16
I32 = mybir.dt.int32

P = 128
CHUNK = 512
BLOCKS = CHUNK // P
HEADS = 2
DH = 64
SCALE = DH ** -0.5
SLOPE = 0.01
EPS = 1e-5
MASKED = -(2.0 ** 100)
LIMIT = 2.0 ** 14
LIFT = 10.0
STEP = 2
WARM_BANKS = 6


def gnn_layer(nc, x, adj, wq, wk, wv, weightr, weightd, bias, out):
    N, D = x.shape
    TILES = N // P
    PAIRS = TILES // 2
    CH = N // CHUNK
    STEPS = CH // STEP
    WIDTH = STEP * CHUNK
    PAIR_STEPS = 4 * STEPS
    AHEAD = 2 * CH
    TURN_AHEAD = 2
    assert D == P and HEADS * DH == P and STEPS == 4

    x_tiles = x.rearrange("(t p) d -> p t d", p=P)
    adj_tiles = adj.rearrange("(t p) m -> p t m", p=P)
    out_tiles = out.rearrange("(t p) d -> p t d", p=P)
    X_LOADS = 4

    with ExitStack() as ctx:
        def sb(name, shape, dt):
            return ctx.enter_context(nc.sbuf_tensor(name, shape, dt))

        def sem(name):
            return ctx.enter_context(nc.semaphore(name))

        x_rows = sb("x_rows", [P, TILES, P], F32)
        x_cols = sb("x_cols", [P, N], F32)
        w_qk = sb("w_qk", [P, 2, HEADS, 2, DH], F32)
        w_v = sb("w_v", [P, P], F32)
        w_out = sb("w_out", [P, 2, P], F32)
        bias_rows = sb("bias_rows", [P, P], F32)
        ident = sb("ident", [P, P], F32)
        q_split = sb("q_split", [P, HEADS, N], F16)
        k_hi = sb("k_hi", [P, HEADS, N], F16)
        k_lo = sb("k_lo", [P, HEADS, N], F16)
        v_split = sb("v_split", [P, TILES, HEADS, 2, DH], F16)
        adj_in = sb("adj_in", [P, 2, N], I32)
        mask = sb("mask", [P, 2, N], BF16)
        rows = sb("rows", [P, HEADS, N], F32)
        p_hi = sb("p_hi", [P, 4, WIDTH], F16)
        p_lo = sb("p_lo", [P, 4, WIDTH], F16)
        maxes = sb("maxes", [P, HEADS, CH], F32)
        top = sb("top", [P, HEADS], F32)
        shift = sb("shift", [P, HEADS], F32)
        sums = sb("sums", [P, 2, HEADS, STEPS], F32)
        total = sb("total", [P, 2, HEADS], F32)
        inverse = sb("inverse", [P, 2, HEADS], F32)
        side = sb("side", [P, HEADS, DH], F32)
        sat = sb("sat", [P, HEADS * DH], F32)
        sat_cols = sb("sat_cols", [P, P], F32)
        projected_sat = sb("projected_sat", [P, P], F32)
        linear = sb("linear", [P, P], F32)
        active = sb("active", [P, P], F32)
        resid = sb("resid", [P, 2, P], F32)
        stats = sb("stats", [P, 6], F32)
        moments = sb("moments", [P, 2, 2], F32)
        rstd = sb("rstd", [P, 2], F32)
        offset = sb("offset", [P, 2], F32)
        power = sb("power", [P, 1], F32)
        normed = sb("normed", [P, 2, P], F32)
        peaks = sb("peaks", [P, 8], F32)
        peaks_all = sb("peaks_all", [P, 8], F32)
        x_peak = sb("x_peak", [P, 1], F32)
        bounds = sb("bounds", [P, 3], F32)
        pow2 = sb("pow2", [P, 3], F32)
        recip2 = sb("recip2", [P, 3], F32)
        factors = sb("factors", [P, 3], F32)
        qk_pow2 = sb("qk_pow2", [P, 1], F32)
        exp_scale = sb("exp_scale", [P, 1], F32)
        neg_scale = sb("neg_scale", [P, 1], F32)
        v_back = sb("v_back", [P, 1], F32)

        ps = ctx.enter_context(nc.psum_tensor("ps", [P, 8, CHUNK], F32))
        SCORE, TURN, SAT = 0, 2, 6
        SIDE_T, SIDE_P = P, 2 * P

        x_loaded = [sem(f"x_loaded{i}") for i in range(X_LOADS)]
        weights_loaded = sem("weights_loaded")
        ends_loaded = sem("ends_loaded")
        adj_loaded = [sem(f"adj_loaded{i}") for i in range(2)]
        ident_ready = sem("ident_ready")
        power_ready = sem("power_ready")
        peaks_ready = sem("peaks_ready")
        peaks_shared = sem("peaks_shared")
        setup = sem("setup")
        x_turned = sem("x_turned")
        x_taken = sem("x_taken")
        projected = sem("projected")
        hi_split = sem("hi_split")
        lo_split = sem("lo_split")
        masked = sem("masked")
        scored = sem("scored")
        scores_taken = sem("scores_taken")
        tops_ready = sem("tops_ready")
        shifts_ready = sem("shifts_ready")
        probs_ready = sem("probs_ready")
        turned = sem("turned")
        hi_ready = sem("hi_ready")
        lo_ready = sem("lo_ready")
        attended = sem("attended")
        totals_ready = sem("totals_ready")
        inverse_ready = sem("inverse_ready")
        side_ready = sem("side_ready")
        merged = sem("merged")
        sat_turned = sem("sat_turned")
        sat_ready = sem("sat_ready")
        sat_projected = sem("sat_projected")
        projection_ready = sem("projection_ready")
        linear_ready = sem("linear_ready")
        active_ready = sem("active_ready")
        resid_ready = sem("resid_ready")
        stats_ready = sem("stats_ready")
        moments_ready = sem("moments_ready")
        rstd_ready = sem("rstd_ready")
        offset_ready = sem("offset_ready")
        normed_ready = sem("normed_ready")
        stored = [sem(f"stored{i}") for i in range(2)]

        SETUP_STEPS = 11
        carrier = {name: sem(f"carrier_{name}") for name in ("DVE", "Pool")}

        def wait(eng, s, value):
            if not isinstance(value, int) or value > 0:
                eng.wait_ge(s, value)

        jobs = [("q", 0, 0)] + [("k", 0, c) for c in range(CH)]
        jobs += [("q", 1, 0)] + [("k", 1, c) for c in range(CH)]
        early = len(jobs)
        jobs += [("v", 0, c) for c in range(CH)]
        jobs += [("q", h, c) for c in range(1, CH) for h in range(HEADS)]
        warm = [("job", n) for n in range(early)]
        for i in range(max(len(jobs) - early, AHEAD)):
            if i < len(jobs) - early:
                warm.append(("job", early + i))
            if i < AHEAD:
                warm.append(("score", i))

        def wait_apart(eng, s, value):
            eng.wait_ge(s, value)
            if not isinstance(value, int):
                eng.sem_inc(carrier[eng.engine.name], 1)

        def turned_probs(s):
            bank = TURN + STEP * (s % 2)
            return ps[:, bank:bank + STEP, :].rearrange("p b c -> p (b c)")

        def warm_bank(n):
            return 2 + (n + CH) % WARM_BANKS

        x_flat = x_rows[:, :, :].rearrange("p t d -> p (t d)")

        block = ctx.enter_context(nc.Block())

        @block.sync
        def _(sp):
            def load_adj(t, q, par):
                wait(sp, masked, STEPS * (t - 1) if not isinstance(t, int) or t >= 2 else 0)
                sp.dma_start(adj_in[:, par, :], adj_tiles[:, t, :]).then_inc(adj_loaded[par], 16)

            def store(t, par):
                sp.wait_ge(normed_ready, t + 1)
                sp.dma_start(out_tiles[:, t, :], normed[:, par, :]).then_inc(stored[par], 16)

            for r in range(2):
                sp.dma_start(w_qk[:, 0, :, r, :], wq.rearrange("i (h d) -> i h d", h=HEADS)).then_inc(weights_loaded, 16)
                sp.dma_start(w_qk[:, 1, :, r, :], wk.rearrange("i (h d) -> i h d", h=HEADS)).then_inc(weights_loaded, 16)
            sp.dma_start(w_v[:, :], wv).then_inc(weights_loaded, 16)
            per = TILES // X_LOADS
            for i in range(X_LOADS):
                sp.dma_start(x_rows[:, i * per:(i + 1) * per, :], x_tiles[:, i * per:(i + 1) * per, :])\
                  .then_inc(x_loaded[i], 16)
            sp.dma_start(w_out[:, 0, :], weightr).then_inc(ends_loaded, 16)
            sp.dma_start(w_out[:, 1, :], weightd).then_inc(ends_loaded, 16)
            sp.dma_start(bias_rows[:, :], bias.partition_broadcast(P)).then_inc(ends_loaded, 16)

            LAG = 5
            for t in range(6):
                load_adj(t, t // 2, t % 2)
                if t >= LAG:
                    store(t - LAG, (t - LAG) % 2)
            with sp.Fori(3, PAIRS) as q:
                for r in range(2):
                    load_adj(2 * q + r, q, r)
                    store(2 * q + r - LAG, (r - LAG) % 2)
            for t in range(TILES - LAG, TILES):
                store(t, t % 2)
            sp.wait_ge(stored[0], 16 * PAIRS)
            sp.wait_ge(stored[1], 16 * PAIRS)

        @block.gpsimd
        def _(pool):
            nc.gpsimd.memset(ident[:, :], 0.0).then_inc(ident_ready, 1)
            pool.wait_ge(ident_ready, 1)
            nc.gpsimd.affine_select(out=ident[:, :], in_=ident[:, :], compare_op=ALU.not_equal, fill=1.0,
                                    base=0, pattern=[[-1, P]], channel_multiplier=1).then_inc(ident_ready, 1)
            nc.gpsimd.memset(power[:, :], -0.5).then_inc(power_ready, 1)
            pool.wait_ge(peaks_ready, X_LOADS + 4)
            nc.gpsimd.partition_all_reduce(peaks_all[:, :], peaks[:, :], P, bass.bass_isa.ReduceOp.max)\
              .then_inc(peaks_shared, 1)

            def make_mask(t, q, par, part):
                if part == 0:
                    if not isinstance(t, int) or t >= 2:
                        wait_apart(pool, scores_taken, 2 * CH * (t - 1))
                    wait_apart(pool, adj_loaded[par], 16 * (q + 1))
                c = slice(part * WIDTH, (part + 1) * WIDTH)
                nc.gpsimd.tensor_scalar(mask[:, par, c], adj_in[:, par, c], 0.0, MASKED, ALU.is_le, ALU.mult)\
                  .then_inc(masked, 1)

            def add_bias(t):
                pool.wait_ge(projection_ready, t + 1)
                wait(pool, active_ready, t)
                nc.gpsimd.tensor_tensor(linear[:, :], projected_sat[:, :], bias_rows[:, :], ALU.add)\
                  .then_inc(linear_ready, 1)

            def add_x(t, par):
                pool.wait_ge(active_ready, t + 1)
                nc.gpsimd.tensor_tensor(resid[:, par, :], active[:, :], x_flat[:, bass.ds(t * P, P)], ALU.add)\
                  .then_inc(resid_ready, 1)

            def inverse_deviation(t, par):
                pool.wait_ge(moments_ready, 2 * t + 2)
                nc.gpsimd.tensor_tensor(rstd[:, par:par + 1], moments[:, par, 1:2], power[:, :], ALU.pow)\
                  .then_inc(rstd_ready, 1)

            def mask_pair(q):
                for r in range(2):
                    t = 2 * q + r
                    first = isinstance(t, int) and t < 4
                    for part in range(STEPS):
                        make_mask(t, q, r, part)
                        if part == 1 and not (first and t < 3):
                            add_bias(t - 3)
                        if part == 2 and not first:
                            inverse_deviation(t - 4, r)
                        if part == 3 and not (first and t < 3):
                            add_x(t - 3, 1 - r)

            pool.wait_ge(power_ready, 1)
            pool.wait_ge(ends_loaded, 16 * 3)
            mask_pair(0)
            mask_pair(1)
            with pool.Fori(2, PAIRS) as q:
                mask_pair(q)
            for t in range(TILES, TILES + 4):
                if t < TILES + 3:
                    add_bias(t - 3)
                inverse_deviation(t - 4, t % 2)
                if t < TILES + 3:
                    add_x(t - 3, (t - 3) % 2)

        @block.scalar
        def _(act):
            def shift_of(unit, h):
                act.wait_ge(tops_ready, unit + 1)
                nc.scalar.activation(shift[:, h:h + 1], top[:, h:h + 1], ACT.Copy, bias=LIFT, scale=neg_scale[:, :])\
                  .then_inc(shifts_ready, 1)

            def exps(unit, h, tile_par, part):
                if part == 0:
                    act.wait_ge(shifts_ready, unit + 1)
                c = slice(part * WIDTH, (part + 1) * WIDTH)
                nc.scalar.activation(rows[:, h, c], rows[:, h, c], ACT.Exp, bias=shift[:, h:h + 1],
                                     scale=exp_scale[:, :], accum_out=sums[:, tile_par, h, part:part + 1])\
                  .then_inc(probs_ready, 1)

            def upper_part(n, s):
                act.wait_ge(turned, n + 1)
                wait(act, attended, n - 3)
                nc.scalar.copy(p_hi[:, s % 4, :], turned_probs(s)).then_inc(hi_ready, 1)

            def side_of(unit, h, tile, par):
                act.wait_ge(attended, STEPS * (unit + 1))
                act.wait_ge(inverse_ready, tile + 1)
                nc.scalar.mul(side[:, h, :], ps[:, SAT + h, DH:2 * DH], inverse[:, par, h:h + 1]).then_inc(side_ready, 1)

            def normalise(tile, pairs_before, par):
                act.wait_ge(offset_ready, tile + 1)
                wait(act, stored[par], 16 * pairs_before)
                nc.scalar.activation(normed[:, par, :], resid[:, par, :], ACT.Identity, bias=offset[:, par:par + 1],
                                     scale=rstd[:, par:par + 1]).then_inc(normed_ready, 1)

            def projection_copy(tile):
                act.wait_ge(sat_projected, tile + 1)
                wait(act, linear_ready, tile)
                nc.scalar.copy(projected_sat[:, :], ps[:, SAT + 1, SIDE_P:SIDE_P + P]).then_inc(projection_ready, 1)

            def sat_copy(tile):
                act.wait_ge(sat_turned, tile + 1)
                nc.scalar.copy(sat_cols[:, :], ps[:, SAT + 1, SIDE_T:SIDE_T + P]).then_inc(sat_ready, 1)

            for n in range(CH):
                act.wait_ge(x_turned, n + 1)
                nc.scalar.copy(x_cols[:, n * CHUNK:(n + 1) * CHUNK], ps[:, 2 + n % WARM_BANKS, :]).then_inc(x_taken, 1)
            act.wait_ge(setup, SETUP_STEPS)
            exp_at = {CH + 1 + 2 * k: k for k in range(STEPS)}
            for kind, n in warm:
                if kind == "job":
                    what, h, c = jobs[n]
                    act.wait_ge(projected, n + 1)
                    src = ps[:, warm_bank(n), :]
                    cols = slice(c * CHUNK, (c + 1) * CHUNK)
                    if what == "q":
                        nc.scalar.mul(q_split[:, h, cols], src, factors[:, 0:1]).then_inc(hi_split, 1)
                    elif what == "k":
                        nc.scalar.mul(k_hi[:, h, cols], src, factors[:, 1:2]).then_inc(hi_split, 1)
                    else:
                        dst = v_split[:, c * BLOCKS:(c + 1) * BLOCKS, :, 0, :].rearrange("p t h d -> p (t h) d")
                        nc.scalar.mul(dst, src.rearrange("p (a d) -> p a d", d=DH), factors[:, 2:3]).then_inc(hi_split, 1)
                elif n == CH:
                    shift_of(0, 0)
                elif n in exp_at:
                    exps(0, 0, 0, exp_at[n])
            for n in range(TURN_AHEAD):
                upper_part(n, n)

            def pair(p, first, last):
                for s in range(PAIR_STEPS):
                    k, i = divmod(s, STEPS)
                    h, r = k % 2, k // 2
                    n, unit, tile = p * PAIR_STEPS + s, 4 * p + k, 2 * p + r
                    ahead = s + TURN_AHEAD
                    if h == 0 and not (first and k == 0):
                        if i == 2:
                            sat_copy(tile - 1)
                        if i == 3:
                            projection_copy(tile - 1)
                    if i == 0 and ahead < PAIR_STEPS:
                        upper_part(n + TURN_AHEAD, ahead)
                    if h == 0 and i == 0 and not (first and k == 0):
                        side_of(unit - 1, 1, tile - 1, 1 - r)
                    if h == 1 and i == 1:
                        side_of(unit - 1, 0, tile, r)
                    if not (last and k == 3):
                        if i == 0:
                            shift_of(unit + 1, 1 - h)
                        exps(unit + 1, 1 - h, (k + 1) // 2 % 2, i)
                    if i > 0 and not (last and ahead >= PAIR_STEPS):
                        upper_part(n + TURN_AHEAD, ahead)
                    if h == 1 and i == 3 and not (first and r < 2):
                        normalise(tile - 2, p - 1, r)

            pair(0, True, False)
            pair(1, False, False)
            with act.Fori(2, PAIRS - 1) as p:
                pair(p, False, False)
            pair(PAIRS - 1, False, True)
            side_of(2 * TILES - 1, 1, TILES - 1, 1)
            sat_copy(TILES - 1)
            projection_copy(TILES - 1)
            normalise(TILES - 2, PAIRS - 1, 0)
            normalise(TILES - 1, PAIRS - 1, 1)

        @block.vector
        def _(dve):
            def mask_max(g, h, tile, tile_par, j, slot, before):
                if h == 0 and j % STEP == 0:
                    dve.wait_ge(masked, STEPS * tile + j // STEP + 1)
                wait(dve, turned, before + 1)
                wait_apart(dve, scored, g + 1)
                c = slice(j * CHUNK, (j + 1) * CHUNK)
                nc.vector.tensor_tensor_reduce(out=rows[:, h, c], in0=ps[:, SCORE + slot, :], in1=mask[:, tile_par, c],
                                               scale=1.0, scalar=2 * MASKED, op0=ALU.add, op1=ALU.max,
                                               accum_out=maxes[:, h, j:j + 1]).then_inc(scores_taken, 1)

            def top_of(unit, h):
                dve.wait_ge(scores_taken, CH * (unit + 1))
                nc.vector.tensor_reduce(top[:, h:h + 1], maxes[:, h, :], AX.X, ALU.max).then_inc(tops_ready, 1)

            def lower_part(n, s):
                dve.wait_ge(hi_ready, n + 1)
                nc.vector.tensor_tensor(p_lo[:, s % 4, :], turned_probs(s), p_hi[:, s % 4, :], ALU.subtract)\
                  .then_inc(lo_ready, 1)

            def sum_up(unit, tile, par):
                dve.wait_ge(probs_ready, STEPS * (unit + 1))
                nc.vector.tensor_reduce(total[:, par, :], sums[:, par, :, :], AX.X, ALU.add).then_inc(totals_ready, 1)

            def invert_sums(tile, par):
                dve.wait_ge(totals_ready, tile + 1)
                nc.vector.reciprocal(inverse[:, par, :], total[:, par, :]).then_inc(inverse_ready, 1)

            def merge(unit, h, tile, par):
                dve.wait_ge(side_ready, unit + 1)
                if h == 0:
                    wait(dve, sat_turned, tile)
                nc.vector.scalar_tensor_tensor(out=sat[:, h * DH:(h + 1) * DH], in0=ps[:, SAT + h, 0:DH],
                                               scalar=inverse[:, par, h:h + 1], in1=side[:, h, :],
                                               op0=ALU.mult, op1=ALU.add).then_inc(merged, 1)

            def leaky(tile):
                dve.wait_ge(linear_ready, tile + 1)
                wait(dve, resid_ready, tile)
                nc.vector.scalar_tensor_tensor(out=active[:, :], in0=linear[:, :], scalar=SLOPE, in1=linear[:, :],
                                               op0=ALU.mult, op1=ALU.max).then_inc(active_ready, 1)

            def statistics(tile, par):
                wait_apart(dve, resid_ready, tile + 1)
                nc.vector.bn_stats(stats[:, :], resid[:, par, :]).then_inc(stats_ready, 1)

            def mean_variance(tile, par):
                wait_apart(dve, stats_ready, tile + 1)
                nc.vector.bn_aggr(moments[:, par, :], stats[:, :]).then_inc(moments_ready, 1)

            def add_eps(tile, par):
                dve.wait_ge(moments_ready, 2 * tile + 1)
                nc.vector.tensor_scalar(moments[:, par, 1:2], moments[:, par, 1:2], EPS, None, ALU.add)\
                  .then_inc(moments_ready, 1)

            def offset_of(tile, par):
                dve.wait_ge(rstd_ready, tile + 1)
                nc.vector.scalar_tensor_tensor(out=offset[:, par:par + 1], in0=moments[:, par, 0:1], scalar=-1.0,
                                               in1=rstd[:, par:par + 1], op0=ALU.mult, op1=ALU.mult)\
                  .then_inc(offset_ready, 1)

            nc.vector.memset(peaks[:, 7:8], 0.0).then_inc(peaks_ready, 1)
            dve.wait_ge(weights_loaded, 16 * 5)
            for i in range(2):
                nc.vector.tensor_reduce(peaks[:, 4 + i:5 + i], w_qk[:, i, :, 0, :], AX.XY, ALU.max,
                                        apply_absolute_value=True).then_inc(peaks_ready, 1)
            nc.vector.tensor_reduce(peaks[:, 6:7], w_v[:, :], AX.X, ALU.max, apply_absolute_value=True)\
              .then_inc(peaks_ready, 1)
            per = TILES // X_LOADS * P
            for i in range(X_LOADS):
                dve.wait_ge(x_loaded[i], 16)
                nc.vector.tensor_reduce(peaks[:, i:i + 1], x_flat[:, i * per:(i + 1) * per], AX.X, ALU.max,
                                        apply_absolute_value=True).then_inc(peaks_ready, 1)
            dve.wait_ge(peaks_shared, 1)
            nc.vector.tensor_reduce(x_peak[:, :], peaks_all[:, 0:X_LOADS], AX.X, ALU.max).then_inc(setup, 1)
            dve.wait_ge(setup, 1)
            nc.vector.tensor_scalar(bounds[:, :], peaks_all[:, 4:7], x_peak[:, :], float(D), ALU.mult, ALU.mult)\
              .then_inc(setup, 1)
            dve.wait_ge(setup, 2)
            nc.vector.tensor_scalar(recip2[:, :], bounds[:, :], 2.0 ** -60, None, ALU.max).then_inc(setup, 1)
            dve.wait_ge(setup, 3)
            nc.vector.tensor_scalar(pow2[:, :].bitcast(I32), recip2[:, :].bitcast(I32), 0x7F800000, None,
                                    ALU.bitwise_and).then_inc(setup, 1)
            dve.wait_ge(setup, 4)
            nc.vector.reciprocal(recip2[:, :], pow2[:, :]).then_inc(setup, 1)
            dve.wait_ge(setup, 5)
            nc.vector.tensor_scalar(factors[:, :], recip2[:, :], LIMIT, None, ALU.mult).then_inc(setup, 1)
            nc.vector.tensor_tensor(qk_pow2[:, :], pow2[:, 0:1], pow2[:, 1:2], ALU.mult).then_inc(setup, 1)
            dve.wait_ge(setup, 7)
            nc.vector.tensor_scalar(exp_scale[:, :], qk_pow2[:, :], SCALE / LIMIT ** 2, None, ALU.mult).then_inc(setup, 1)
            nc.vector.tensor_scalar(neg_scale[:, :], qk_pow2[:, :], -SCALE / LIMIT ** 2, None, ALU.mult)\
              .then_inc(setup, 1)
            nc.vector.tensor_scalar(v_back[:, :], pow2[:, 2:3], 1.0 / LIMIT, None, ALU.mult).then_inc(setup, 1)
            dve.wait_ge(setup, 10)
            dve.wait_ge(ends_loaded, 16 * 3)
            nc.vector.tensor_scalar(w_out[:, :, :], w_out[:, :, :], v_back[:, :], None, ALU.mult).then_inc(setup, 1)

            for kind, n in warm:
                if kind == "job":
                    what, h, c = jobs[n]
                    dve.wait_ge(hi_split, n + 1)
                    cols = slice(c * CHUNK, (c + 1) * CHUNK)
                    if what == "q":
                        part = q_split[DH:P, h, cols]
                        nc.vector.scalar_tensor_tensor(out=part, in0=ps[DH:P, warm_bank(n), :], scalar=factors[DH:P, 0:1],
                                                       in1=part, op0=ALU.mult, op1=ALU.subtract).then_inc(lo_split, 1)
                    elif what == "k":
                        nc.vector.scalar_tensor_tensor(out=k_lo[:, h, cols], in0=ps[:, warm_bank(n), :],
                                                       scalar=factors[:, 1:2], in1=k_hi[:, h, cols],
                                                       op0=ALU.mult, op1=ALU.subtract).then_inc(lo_split, 1)
                    else:
                        v = v_split[:, c * BLOCKS:(c + 1) * BLOCKS, :, :, :].rearrange("p t h s d -> p (t h) s d")
                        nc.vector.scalar_tensor_tensor(
                            out=v[:, :, 1, :], in0=ps[:, warm_bank(n), :].rearrange("p (a d) -> p a d", d=DH),
                            scalar=factors[:, 2:3], in1=v[:, :, 0, :], op0=ALU.mult, op1=ALU.subtract)\
                          .then_inc(lo_split, 1)
                else:
                    h, j = divmod(n, CH)
                    mask_max(n, h, 0, 0, j, n % 2, -1)
                    if n == CH - 1:
                        top_of(0, 0)
            lower_part(0, 0)

            def pair(p, first, last):
                for s in range(PAIR_STEPS):
                    k, i = divmod(s, STEPS)
                    h, r = k % 2, k // 2
                    n, unit, tile = p * PAIR_STEPS + s, 4 * p + k, 2 * p + r
                    if not (last and k >= 2):
                        mask_max(STEP * n + AHEAD, h, tile + 1, 1 - r, STEP * i, 0, n)
                    if i == 0 and not (last and k == 3):
                        top_of(unit + 1, 1 - h)
                    if i == 0 and h == 1:
                        sum_up(unit, tile, r)
                    if not (last and s + 1 >= PAIR_STEPS):
                        lower_part(n + 1, s + 1)
                    if i == 0 and h == 1:
                        invert_sums(tile, r)
                    if not (last and k >= 2):
                        mask_max(STEP * n + AHEAD + 1, h, tile + 1, 1 - r, STEP * i + 1, 1, n)
                    if h == 0 and i == 0 and not (first and k == 0):
                        merge(unit - 1, 1, tile - 1, 1 - r)
                    if h == 1 and i == 1:
                        merge(unit - 1, 0, tile, r)
                    if h == 1 and i == 2 and not (first and r == 0):
                        leaky(tile - 1)
                    if not first:
                        if h == 0 and i == 1:
                            statistics(tile - 2, r)
                        if h == 0 and i == 2:
                            mean_variance(tile - 2, r)
                        if h == 0 and i == 3:
                            add_eps(tile - 2, r)
                        if h == 1 and i == 2:
                            offset_of(tile - 2, r)

            pair(0, True, False)
            with dve.Fori(1, PAIRS - 1) as p:
                pair(p, False, False)
            pair(PAIRS - 1, False, True)
            merge(2 * TILES - 1, 1, TILES - 1, 1)
            for t in (TILES - 2, TILES - 1):
                if t == TILES - 1:
                    leaky(t)
                statistics(t, t % 2)
                mean_variance(t, t % 2)
                add_eps(t, t % 2)
                offset_of(t, t % 2)

        @block.tensor
        def _(pe):
            def score(g, h, tile, j, slot):
                wait(pe, scores_taken, g - 1)
                lhsT = q_split[:, h, bass.ds(tile * P, P)]
                c = slice(j * CHUNK, (j + 1) * CHUNK)
                nc.tensor.matmul(ps[:, SCORE + slot, :], lhsT, k_hi[:, h, c], start=True, stop=False)
                nc.tensor.matmul(ps[:, SCORE + slot, :], lhsT, k_lo[:, h, c], start=False, stop=True).then_inc(scored, 1)

            def turn(n, s, unit, h):
                i = s % STEPS
                pe.wait_ge(probs_ready, STEPS * unit + i + 1)
                wait(pe, lo_ready, n - 1)
                for b in range(STEP * BLOCKS):
                    c = slice(i * WIDTH + b * P, i * WIDTH + (b + 1) * P)
                    last = nc.tensor.transpose(turned_probs(s)[:, b * P:(b + 1) * P], rows[:, h, c], ident[:, :])
                last.then_inc(turned, 1)

            def attend(n, s, unit, tile, h, half):
                i = s % STEPS
                if half == 0:
                    pe.wait_ge(lo_ready, n + 1)
                if half == 0 and i == 0:
                    wait(pe, merged, unit - 1)
                    if h == 1:
                        wait(pe, projection_ready, tile)
                for b in range(half * BLOCKS, (half + 1) * BLOCKS):
                    c = slice(b * P, (b + 1) * P)
                    v = v_split[:, i * STEP * BLOCKS + b, h, :, :].rearrange("p s d -> p (s d)")
                    nc.tensor.matmul(ps[:, SAT + h, 0:2 * DH], p_hi[:, s % 4, c], v,
                                     start=(i == 0 and b == 0), stop=False, skip_group_check=True)
                    last = nc.tensor.matmul(ps[:, SAT + h, 0:DH], p_lo[:, s % 4, c], v[:, 0:DH], start=False,
                                            stop=(i == STEPS - 1 and b == STEP * BLOCKS - 1), skip_group_check=True)
                if half == STEP - 1:
                    last.then_inc(attended, 1)

            def turn_sat(tile):
                pe.wait_ge(merged, 2 * tile + 2)
                nc.tensor.transpose(ps[:, SAT + 1, SIDE_T:SIDE_T + P], sat[:, :], ident[:, :]).then_inc(sat_turned, 1)

            def project_sat(tile):
                pe.wait_ge(sat_ready, tile + 1)
                w = w_out[:, :, :].rearrange("p s d -> p (s d)")[:, bass.ds(tile // (TILES // 2) * P, P)]
                nc.tensor.matmul(ps[:, SAT + 1, SIDE_P:SIDE_P + P], sat_cols[:, :], w, start=True, stop=True)\
                  .then_inc(sat_projected, 1)

            pe.wait_ge(ident_ready, 2)
            for n in range(CH):
                if n % 2 == 0:
                    pe.wait_ge(x_loaded[n // 2], 16)
                wait(pe, x_taken, n - WARM_BANKS + 1)
                for b in range(BLOCKS):
                    last = nc.tensor.transpose(ps[:, 2 + n % WARM_BANKS, b * P:(b + 1) * P],
                                               x_rows[:, n * BLOCKS + b, :], ident[:, :])
                last.then_inc(x_turned, 1)
            pe.wait_ge(weights_loaded, 16 * 5)
            for kind, n in warm:
                if kind == "score":
                    h, j = divmod(n, CH)
                    if n == 0:
                        pe.wait_ge(lo_split, early)
                    score(n, h, 0, j, n % 2)
                    continue
                what, h, c = jobs[n]
                if n < WARM_BANKS:
                    pe.wait_ge(x_taken, max(n + CH - WARM_BANKS, c) + 1)
                else:
                    pe.wait_ge(lo_split, n - WARM_BANKS + 1)
                    if n < WARM_BANKS + CH:
                        pe.wait_ge(x_taken, CH)
                bank = warm_bank(n)
                if what == "v":
                    for b in range(BLOCKS):
                        keys = slice(c * CHUNK + b * P, c * CHUNK + (b + 1) * P)
                        last = nc.tensor.matmul(ps[:, bank, b * P:(b + 1) * P], x_cols[:, keys], w_v[:, :],
                                                start=True, stop=True)
                else:
                    w = w_qk[:, 0 if what == "q" else 1, h, :, :].rearrange("p r d -> p (r d)")
                    last = nc.tensor.matmul(ps[:, bank, :], w, x_cols[:, c * CHUNK:(c + 1) * CHUNK], start=True, stop=True)
                last.then_inc(projected, 1)
            pe.wait_ge(lo_split, len(jobs))
            for n in range(TURN_AHEAD):
                turn(n, n, 0, 0)

            def pair(p, last):
                for s in range(PAIR_STEPS):
                    k, i = divmod(s, STEPS)
                    h, r = k % 2, k // 2
                    n, unit, tile = p * PAIR_STEPS + s, 4 * p + k, 2 * p + r
                    if not (last and k >= 2):
                        score(STEP * n + AHEAD, h, tile + 1, STEP * i, 0)
                    if not (last and s + TURN_AHEAD >= PAIR_STEPS):
                        ahead = s + TURN_AHEAD
                        turn(n + TURN_AHEAD, ahead, 4 * p + ahead // STEPS, ahead // STEPS % 2)
                    attend(n, s, unit, tile, h, 0)
                    if not (last and k >= 2):
                        score(STEP * n + AHEAD + 1, h, tile + 1, STEP * i + 1, 1)
                    attend(n, s, unit, tile, h, 1)
                    if h == 0 and not (isinstance(p, int) and p == 0 and k == 0):
                        if i == 1:
                            turn_sat(tile - 1)
                        if i == 2:
                            project_sat(tile - 1)

            pair(0, False)
            with pe.Fori(1, PAIRS - 1) as p:
                pair(p, False)
            pair(PAIRS - 1, True)
            turn_sat(TILES - 1)
            pe.wait_ge(setup, SETUP_STEPS)
            project_sat(TILES - 1)


_INS = ["x", "adj", "L0_gnn_Wq", "L0_gnn_Wk", "L0_gnn_Wv", "L0_gnn_weightr", "L0_gnn_weightd", "L0_gnn_bias"]


def kernel(**inputs):
    import numpy as _np
    import concourse.bacc as _bacc
    from concourse import mybir as _mybir
    from concourse.bass_utils import run_bass_kernel_spmd as _run

    nc = _bacc.Bacc("TRN2", target_bir_lowering=False, num_devices=1)
    arrays, args = {}, []
    for name in _INS:
        a = _np.ascontiguousarray(inputs[name])
        arrays[f"in_{name}_dram"] = a
        args.append(nc.dram_tensor(f"in_{name}_dram", a.shape, _mybir.dt.from_np(a.dtype), kind="ExternalInput").ap())
    shape = inputs["x"].shape
    args.append(nc.dram_tensor("out_0_dram", shape, _mybir.dt.float32, kind="ExternalOutput").ap())
    gnn_layer(nc, *args)
    r = _run(nc, [arrays], core_ids=[0])
    return r.results[0]["out_0_dram"]
```

```python
from contextlib import ExitStack

import concourse.bass as bass
from concourse import mybir

ALU = mybir.AluOpType
ACT = mybir.ActivationFunctionType
AX = mybir.AxisListType
F32 = mybir.dt.float32
F16 = mybir.dt.float16
BF16 = mybir.dt.bfloat16
I32 = mybir.dt.int32

P = 128
CHUNK = 512
BLOCKS = CHUNK // P
HEADS = 2
DH = 64
SCALE = DH ** -0.5
SLOPE = 0.01
EPS = 1e-5
MASKED = -(2.0 ** 100)
LIMIT = 2.0 ** 14
LIFT = 10.0
STEP = 2
WARM_BANKS = 6


def gnn_layer(nc, x, adj, wq, wk, wv, weightr, weightd, bias, out):
    N, D = x.shape
    TILES = N // P
    PAIRS = TILES // 2
    CH = N // CHUNK
    STEPS = CH // STEP
    WIDTH = STEP * CHUNK
    PAIR_STEPS = 4 * STEPS
    AHEAD = 2 * CH
    TURN_AHEAD = 2
    assert D == P and HEADS * DH == P and STEPS == 4

    x_tiles = x.rearrange("(t p) d -> p t d", p=P)
    adj_tiles = adj.rearrange("(t p) m -> p t m", p=P)
    out_tiles = out.rearrange("(t p) d -> p t d", p=P)
    X_LOADS = 4

    with ExitStack() as ctx:
        def sb(name, shape, dt):
            return ctx.enter_context(nc.sbuf_tensor(name, shape, dt))

        def sem(name):
            return ctx.enter_context(nc.semaphore(name))

        x_rows = sb("x_rows", [P, TILES, P], F32)
        x_cols = sb("x_cols", [P, N], F32)
        w_in = sb("w_in", [P, 3, P], F32)
        w_q_twice = sb("w_q_twice", [P, HEADS, 2, DH], F32)
        w_out = sb("w_out", [P, 2, P], F32)
        bias_rows = sb("bias_rows", [P, P], F32)
        ident = sb("ident", [P, P], F32)
        q_hi = sb("q_hi", [P, HEADS, N], F16)
        q_lo = sb("q_lo", [P, HEADS, N], F16)
        k_split = sb("k_split", [P, HEADS, N], F16)
        v_split = sb("v_split", [P, TILES, HEADS, 2, DH], F16)
        adj_in = sb("adj_in", [P, 2, N], I32)
        mask = sb("mask", [P, 2, N], BF16)
        rows = sb("rows", [P, HEADS, N], F32)
        p_hi = sb("p_hi", [P, 4, WIDTH], F16)
        p_lo = sb("p_lo", [P, 4, WIDTH], F16)
        k_hi_stage = p_hi[:, :, :].rearrange("p s c -> p (s c)")
        k_lo_stage = p_lo[:, :, :].rearrange("p s c -> p (s c)")
        q_stage = x_cols[:, :].bitcast(F16).rearrange("p (c s k) -> p c s k", s=2, k=CHUNK)
        maxes = sb("maxes", [P, HEADS, CH], F32)
        top = sb("top", [P, HEADS], F32)
        shift = sb("shift", [P, HEADS], F32)
        sums = sb("sums", [P, 2, HEADS, STEPS], F32)
        total = sb("total", [P, 2, HEADS], F32)
        inverse = sb("inverse", [P, 2, HEADS], F32)
        summands = sb("summands", [P, HEADS, 2, DH], F32)
        sat = sb("sat", [P, HEADS * DH], F32)
        sat_cols = sb("sat_cols", [P, P], F32)
        projected_sat = sb("projected_sat", [P, P], F32)
        linear = sb("linear", [P, P], F32)
        active = sb("active", [P, P], F32)
        resid = sb("resid", [P, 2, P], F32)
        stats = sb("stats", [P, 6], F32)
        moments = sb("moments", [P, 2, 2], F32)
        rstd = sb("rstd", [P, 2], F32)
        offset = sb("offset", [P, 2], F32)
        power = sb("power", [P, 1], F32)
        normed = sb("normed", [P, 2, P], F32)
        peaks = sb("peaks", [P, 8], F32)
        peaks_all = sb("peaks_all", [P, 8], F32)
        x_peak = sb("x_peak", [P, 1], F32)
        bounds = sb("bounds", [P, 3], F32)
        pow2 = sb("pow2", [P, 3], F32)
        recip2 = sb("recip2", [P, 3], F32)
        factors = sb("factors", [P, 3], F32)
        qk_pow2 = sb("qk_pow2", [P, 1], F32)
        exp_scale = sb("exp_scale", [P, 1], F32)
        neg_scale = sb("neg_scale", [P, 1], F32)
        v_back = sb("v_back", [P, 1], F32)

        ps = ctx.enter_context(nc.psum_tensor("ps", [P, 8, CHUNK], F32))
        SCORE, TURN, SAT = 0, 2, 6
        SIDE_T, SIDE_P = P, 2 * P

        x_loaded = [sem(f"x_loaded{i}") for i in range(X_LOADS)]
        weights_loaded = sem("weights_loaded")
        twice_loaded = sem("twice_loaded")
        ends_loaded = sem("ends_loaded")
        adj_loaded = [sem(f"adj_loaded{i}") for i in range(2)]
        ident_ready = sem("ident_ready")
        power_ready = sem("power_ready")
        peaks_ready = sem("peaks_ready")
        peaks_shared = sem("peaks_shared")
        w_out_ready = sem("w_out_ready")
        setup = sem("setup")
        x_turned = sem("x_turned")
        x_taken = sem("x_taken")
        projected = sem("projected")
        hi_split = sem("hi_split")
        lo_split = sem("lo_split")
        k_placed = [sem(f"k_placed{i}") for i in range(STEPS)]
        k_placed_second = sem("k_placed_second")
        q_placed = sem("q_placed")
        masked = sem("masked")
        scored = sem("scored")
        scores_taken = sem("scores_taken")
        tops_ready = sem("tops_ready")
        shifts_ready = sem("shifts_ready")
        probs_ready = sem("probs_ready")
        turned = sem("turned")
        hi_ready = sem("hi_ready")
        lo_ready = sem("lo_ready")
        attended = sem("attended")
        totals_ready = sem("totals_ready")
        inverse_ready = sem("inverse_ready")
        scaled = sem("scaled")
        merged = sem("merged")
        sat_turned = sem("sat_turned")
        sat_ready = sem("sat_ready")
        sat_projected = sem("sat_projected")
        projection_ready = sem("projection_ready")
        linear_ready = sem("linear_ready")
        active_ready = sem("active_ready")
        resid_ready = sem("resid_ready")
        stats_ready = sem("stats_ready")
        moments_ready = sem("moments_ready")
        rstd_ready = sem("rstd_ready")
        offset_ready = sem("offset_ready")
        normed_ready = sem("normed_ready")
        stored = [sem(f"stored{i}") for i in range(2)]

        SETUP_STEPS = 10
        carrier = {name: sem(f"carrier_{name}") for name in ("DVE", "Pool")}

        def wait(eng, s, value):
            if not isinstance(value, int) or value > 0:
                eng.wait_ge(s, value)

        jobs = [("q first", 0, 0, 1)] + [("k", None, c, STEP) for c in range(0, CH, STEP)]
        early = len(jobs)
        jobs += [("q first", 1, 0, 1)] + [("v", None, c, STEP) for c in range(0, CH, STEP)]
        jobs += [("q", None, 1, STEP - 1)] + [("q", None, c, STEP) for c in range(STEP, CH, STEP)]
        groups = [[("score", STEP * i + j) for j in range(STEP)] for i in range(AHEAD // STEP)]
        late = [("job", n) for n in range(early, len(jobs))]
        assert len(late) == len(groups) + 1
        warm = [("job", n) for n in range(early)]
        warm_pe = warm + groups[0] + late[:1]
        for i, group in enumerate(groups):
            warm = warm + group + late[i:i + 1]
            if i > 0:
                warm_pe = warm_pe + late[i:i + 1] + group
        warm, warm_pe = warm + late[-1:], warm_pe + late[-1:]

        def wait_apart(eng, s, value):
            eng.wait_ge(s, value)
            if not isinstance(value, int):
                eng.sem_inc(carrier[eng.engine.name], 1)

        SHARED = (2 * STEPS + 3, 3 * STEPS + 1)

        def turned_probs(s):
            bank = TURN + STEP * (s % 2)
            return ps[:, bank:bank + STEP, :].rearrange("p b c -> p (b c)")

        def bank_of(n):
            return 2 + (2 * n + CH) % WARM_BANKS

        def projection(n, chunks):
            return ps[:, bank_of(n):bank_of(n) + chunks, :].rearrange("p b c -> p (b c)")

        x_flat = x_rows[:, :, :].rearrange("p t d -> p (t d)")

        block = ctx.enter_context(nc.Block())

        @block.sync
        def _(sp):
            def load_adj(t, q, par):
                wait(sp, masked, STEPS * (t - 1) if not isinstance(t, int) or t >= 2 else 0)
                sp.dma_start(adj_in[:, par, :], adj_tiles[:, t, :]).then_inc(adj_loaded[par], 16)

            def store(t, par):
                sp.wait_ge(normed_ready, t + 1)
                sp.dma_start(out_tiles[:, t, :], normed[:, par, :]).then_inc(stored[par], 16)

            per = TILES // X_LOADS
            for i in range(X_LOADS):
                sp.dma_start(x_rows[:, i * per:(i + 1) * per, :], x_tiles[:, i * per:(i + 1) * per, :])\
                  .then_inc(x_loaded[i], 16)
            for i, w in enumerate((wq, wk, wv)):
                sp.dma_start(w_in[:, i, :], w).then_inc(weights_loaded, 16)
            for r in range(2):
                sp.dma_start(w_q_twice[:, :, r, :], wq.rearrange("i (h d) -> i h d", h=HEADS)).then_inc(twice_loaded, 16)
            load_adj(0, 0, 0)
            sp.dma_start(w_out[:, 0, :], weightr).then_inc(ends_loaded, 16)
            sp.dma_start(w_out[:, 1, :], weightd).then_inc(ends_loaded, 16)
            sp.dma_start(bias_rows[:, :], bias.partition_broadcast(P)).then_inc(ends_loaded, 16)

            LAG = 5
            for c in range(0, CH, STEP):
                cols = slice(c * CHUNK, (c + STEP) * CHUNK)
                for half, (ready, stage) in enumerate(((hi_split, k_hi_stage), (lo_split, k_lo_stage))):
                    sp.wait_ge(ready, jobs.index(("k", None, c, STEP)) + 1)
                    sp.dma_start(k_split[half * DH:(half + 1) * DH, 0, cols], stage[0:DH, cols])\
                      .then_inc(k_placed[c // STEP], 16)
                if c == STEP:
                    load_adj(1, 0, 1)
            for half, stage in enumerate((k_hi_stage, k_lo_stage)):
                sp.dma_start(k_split[half * DH:(half + 1) * DH, 1, :], stage[DH:P, :]).then_inc(k_placed_second, 16)
            load_adj(2, 1, 0)
            for part, (ready, q_part) in enumerate(((hi_split, q_hi), (lo_split, q_lo))):
                sp.wait_ge(ready, len(jobs))
                for half in range(2):
                    for h in range(HEADS):
                        sp.dma_start(q_part[half * DH:(half + 1) * DH, h, CHUNK:].rearrange("p (c k) -> p c k", k=CHUNK),
                                     q_stage[h * DH:(h + 1) * DH, 1:, part, :]).then_inc(q_placed, 16)
            for t in range(3, 6):
                load_adj(t, t // 2, t % 2)
                if t >= LAG:
                    store(t - LAG, (t - LAG) % 2)
            with sp.Fori(3, PAIRS) as q:
                for r in range(2):
                    load_adj(2 * q + r, q, r)
                    store(2 * q + r - LAG, (r - LAG) % 2)
            for t in range(TILES - LAG, TILES):
                store(t, t % 2)
            sp.wait_ge(stored[0], 16 * PAIRS)
            sp.wait_ge(stored[1], 16 * PAIRS)

        @block.gpsimd
        def _(pool):
            nc.gpsimd.memset(ident[:, :], 0.0).then_inc(ident_ready, 1)
            pool.wait_ge(ident_ready, 1)
            nc.gpsimd.affine_select(out=ident[:, :], in_=ident[:, :], compare_op=ALU.not_equal, fill=1.0,
                                    base=0, pattern=[[-1, P]], channel_multiplier=1).then_inc(ident_ready, 1)
            nc.gpsimd.memset(power[:, :], -0.5).then_inc(power_ready, 1)
            pool.wait_ge(peaks_ready, X_LOADS + 2)
            nc.gpsimd.partition_all_reduce(peaks_all[:, :], peaks[:, :], P, bass.bass_isa.ReduceOp.max)\
              .then_inc(peaks_shared, 1)

            def make_mask(t, q, par, part, steps):
                if part == 0:
                    if not isinstance(t, int) or t >= 2:
                        wait_apart(pool, scores_taken, 2 * CH * (t - 1))
                    wait_apart(pool, adj_loaded[par], 16 * (q + 1))
                c = slice(part * WIDTH, (part + steps) * WIDTH)
                nc.gpsimd.tensor_scalar(mask[:, par, c], adj_in[:, par, c], 0.0, MASKED, ALU.is_le, ALU.mult)\
                  .then_inc(masked, steps)

            def merge(t):
                pool.wait_ge(scaled, HEADS * (t + 1))
                wait(pool, sat_turned, t)
                nc.gpsimd.tensor_tensor(sat[:, :].rearrange("p (h d) -> p h d", d=DH), summands[:, :, 0, :],
                                        summands[:, :, 1, :], ALU.add).then_inc(merged, 1)

            def add_bias(t):
                pool.wait_ge(projection_ready, t + 1)
                wait(pool, active_ready, t)
                nc.gpsimd.tensor_tensor(linear[:, :], projected_sat[:, :], bias_rows[:, :], ALU.add)\
                  .then_inc(linear_ready, 1)

            def add_x(t, par):
                pool.wait_ge(active_ready, t + 1)
                nc.gpsimd.tensor_tensor(resid[:, par, :], active[:, :], x_flat[:, bass.ds(t * P, P)], ALU.add)\
                  .then_inc(resid_ready, 1)

            def inverse_deviation(t, par):
                pool.wait_ge(moments_ready, 2 * t + 2)
                nc.gpsimd.tensor_tensor(rstd[:, par:par + 1], moments[:, par, 1:2], power[:, :], ALU.pow)\
                  .then_inc(rstd_ready, 1)

            def mask_pair(q):
                for r in range(2):
                    t = 2 * q + r
                    first = isinstance(t, int) and t < 4
                    if isinstance(t, int) and t == 0:
                        pool.wait_ge(masked, STEPS)
                        continue
                    for part, steps in ((0, 1), (1, STEPS - 2), (STEPS - 1, 1)):
                        make_mask(t, q, r, part, steps)
                        if part == 0 and not (first and t < 3):
                            merge(t - 3)
                        if part == 1 and not first:
                            inverse_deviation(t - 4, r)
                        if part == 1 and not (first and t < 3):
                            add_bias(t - 3)
                        if part == STEPS - 1 and not (first and t < 3):
                            add_x(t - 3, 1 - r)

            pool.wait_ge(power_ready, 1)
            pool.wait_ge(ends_loaded, 16 * 3)
            pool.wait_ge(setup, SETUP_STEPS)
            nc.gpsimd.tensor_scalar(w_out[:, :, :], w_out[:, :, :], v_back[:, :], None, ALU.mult).then_inc(w_out_ready, 1)
            mask_pair(0)
            mask_pair(1)
            with pool.Fori(2, PAIRS) as q:
                mask_pair(q)
            for t in range(TILES, TILES + 4):
                if t < TILES + 3:
                    merge(t - 3)
                inverse_deviation(t - 4, t % 2)
                if t < TILES + 3:
                    add_bias(t - 3)
                    add_x(t - 3, (t - 3) % 2)

        @block.scalar
        def _(act):
            def shift_of(unit, h):
                act.wait_ge(tops_ready, unit + 1)
                nc.scalar.activation(shift[:, h:h + 1], top[:, h:h + 1], ACT.Copy, bias=LIFT, scale=neg_scale[:, :])\
                  .then_inc(shifts_ready, 1)

            def exps(unit, h, tile_par, part):
                if part == 0:
                    act.wait_ge(shifts_ready, unit + 1)
                c = slice(part * WIDTH, (part + 1) * WIDTH)
                nc.scalar.activation(rows[:, h, c], rows[:, h, c], ACT.Exp, bias=shift[:, h:h + 1],
                                     scale=exp_scale[:, :], accum_out=sums[:, tile_par, h, part:part + 1])\
                  .then_inc(probs_ready, 1)

            def upper_part(n, s):
                act.wait_ge(turned, n + 1)
                wait(act, attended, n - 3)
                nc.scalar.copy(p_hi[:, s % 4, :], turned_probs(s)).then_inc(hi_ready, 1)

            def scale_sum(unit, h, tile, par):
                act.wait_ge(attended, STEPS * (unit + 1))
                act.wait_ge(inverse_ready, tile + 1)
                wait(act, merged, tile)
                nc.scalar.mul(summands[:, h, :, :].rearrange("p s d -> p (s d)"), ps[:, SAT + h, 0:2 * DH],
                              inverse[:, par, h:h + 1]).then_inc(scaled, 1)

            def normalise(tile, pairs_before, par):
                act.wait_ge(offset_ready, tile + 1)
                wait(act, stored[par], 16 * pairs_before)
                nc.scalar.activation(normed[:, par, :], resid[:, par, :], ACT.Identity, bias=offset[:, par:par + 1],
                                     scale=rstd[:, par:par + 1]).then_inc(normed_ready, 1)

            def projection_copy(tile):
                act.wait_ge(sat_projected, tile + 1)
                wait(act, linear_ready, tile)
                nc.scalar.copy(projected_sat[:, :], ps[:, SAT + 1, SIDE_P:SIDE_P + P]).then_inc(projection_ready, 1)

            def sat_copy(tile):
                act.wait_ge(sat_turned, tile + 1)
                nc.scalar.copy(sat_cols[:, :], ps[:, SAT + 1, SIDE_T:SIDE_T + P]).then_inc(sat_ready, 1)

            for n in range(CH):
                act.wait_ge(x_turned, n + 1)
                nc.scalar.copy(x_cols[:, n * CHUNK:(n + 1) * CHUNK], ps[:, 2 + n % WARM_BANKS, :]).then_inc(x_taken, 1)
            act.wait_ge(setup, SETUP_STEPS)
            exp_at = {CH + 2 + 2 * k: k for k in range(STEPS - 1)}
            for kind, n in warm:
                if kind == "job":
                    what, h, c, chunks = jobs[n]
                    act.wait_ge(projected, n + 1)
                    src = projection(n, chunks)
                    cols = slice(c * CHUNK, (c + chunks) * CHUNK)
                    if what == "q first":
                        nc.scalar.mul(q_hi[:, h, cols], src, factors[:, 0:1]).then_inc(hi_split, 1)
                    elif what == "k":
                        nc.scalar.mul(k_hi_stage[:, cols], src, factors[:, 1:2]).then_inc(hi_split, 1)
                    elif what == "q":
                        nc.scalar.mul(q_stage[:, c:c + chunks, 0, :], src.rearrange("p (c k) -> p c k", k=CHUNK),
                                      factors[:, 0:1]).then_inc(hi_split, 1)
                    else:
                        dst = v_split[:, c * BLOCKS:(c + chunks) * BLOCKS, :, 0, :].rearrange("p t h d -> p (t h) d")
                        nc.scalar.mul(dst, src.rearrange("p (a d) -> p a d", d=DH), factors[:, 2:3]).then_inc(hi_split, 1)
                elif n == CH + 1:
                    shift_of(0, 0)
                elif n in exp_at:
                    exps(0, 0, 0, exp_at[n])
            act.wait_ge(k_placed_second, 16 * 2)
            upper_part(0, 0)
            exps(0, 0, 0, STEPS - 1)
            upper_part(1, 1)

            def pair(p, first, last):
                for s in range(PAIR_STEPS):
                    k, i = divmod(s, STEPS)
                    h, r = k % 2, k // 2
                    n, unit, tile = p * PAIR_STEPS + s, 4 * p + k, 2 * p + r
                    ahead = s + TURN_AHEAD
                    if h == 0 and not (first and k == 0):
                        if i == 3:
                            sat_copy(tile - 1)
                    if h == 1 and i == 0 and not (first and r == 0):
                        projection_copy(tile - 1)
                    if not (last and (ahead >= PAIR_STEPS or ahead in SHARED)):
                        if last and ahead - 1 in SHARED:
                            act.wait_ge(hi_ready, n + TURN_AHEAD)
                        upper_part(n + TURN_AHEAD, ahead)
                    if h == 0 and i == 0 and not (first and k == 0):
                        scale_sum(unit - 1, 1, tile - 1, 1 - r)
                    if h == 1 and i == 1:
                        scale_sum(unit - 1, 0, tile, r)
                    if not (last and k == 3):
                        if i == 0:
                            shift_of(unit + 1, 1 - h)
                        exps(unit + 1, 1 - h, (k + 1) // 2 % 2, i)
                    if h == 1 and i == 3 and not (first and r < 2):
                        normalise(tile - 2, p - 1, r)

            pair(0, True, False)
            pair(1, False, False)
            with act.Fori(2, PAIRS - 1) as p:
                pair(p, False, False)
            pair(PAIRS - 1, False, True)
            scale_sum(2 * TILES - 1, 1, TILES - 1, 1)
            sat_copy(TILES - 1)
            projection_copy(TILES - 1)
            normalise(TILES - 2, PAIRS - 1, 0)
            normalise(TILES - 1, PAIRS - 1, 1)

        @block.vector
        def _(dve):
            def mask_max(g, h, tile, tile_par, j, slot, before):
                if h == 0 and j % STEP == 0:
                    dve.wait_ge(masked, STEPS * tile + j // STEP + 1)
                wait(dve, turned, before + 1)
                wait_apart(dve, scored, g + 1)
                c = slice(j * CHUNK, (j + 1) * CHUNK)
                nc.vector.tensor_tensor_reduce(out=rows[:, h, c], in0=ps[:, SCORE + slot, :], in1=mask[:, tile_par, c],
                                               scale=1.0, scalar=2 * MASKED, op0=ALU.add, op1=ALU.max,
                                               accum_out=maxes[:, h, j:j + 1]).then_inc(scores_taken, 1)

            def top_of(unit, h):
                dve.wait_ge(scores_taken, CH * (unit + 1))
                nc.vector.tensor_reduce(top[:, h:h + 1], maxes[:, h, :], AX.X, ALU.max).then_inc(tops_ready, 1)

            def upper_part(n, s):
                dve.wait_ge(turned, n + 1)
                dve.wait_ge(attended, n - 3)
                dve.wait_ge(hi_ready, n)
                nc.vector.tensor_copy(p_hi[:, s % 4, :], turned_probs(s)).then_inc(hi_ready, 1)

            def lower_part(n, s):
                dve.wait_ge(hi_ready, n + 1)
                nc.vector.tensor_tensor(p_lo[:, s % 4, :], turned_probs(s), p_hi[:, s % 4, :], ALU.subtract)\
                  .then_inc(lo_ready, 1)

            def sum_up(unit, tile, par):
                dve.wait_ge(probs_ready, STEPS * (unit + 1))
                nc.vector.tensor_reduce(total[:, par, :], sums[:, par, :, :], AX.X, ALU.add).then_inc(totals_ready, 1)

            def invert_sums(tile, par):
                dve.wait_ge(totals_ready, tile + 1)
                nc.vector.reciprocal(inverse[:, par, :], total[:, par, :]).then_inc(inverse_ready, 1)

            def leaky(tile):
                dve.wait_ge(linear_ready, tile + 1)
                wait(dve, resid_ready, tile)
                nc.vector.scalar_tensor_tensor(out=active[:, :], in0=linear[:, :], scalar=SLOPE, in1=linear[:, :],
                                               op0=ALU.mult, op1=ALU.max).then_inc(active_ready, 1)

            def statistics(tile, par):
                wait_apart(dve, resid_ready, tile + 1)
                nc.vector.bn_stats(stats[:, :], resid[:, par, :]).then_inc(stats_ready, 1)

            def mean_variance(tile, par):
                wait_apart(dve, stats_ready, tile + 1)
                nc.vector.bn_aggr(moments[:, par, :], stats[:, :]).then_inc(moments_ready, 1)

            def add_eps(tile, par):
                dve.wait_ge(moments_ready, 2 * tile + 1)
                nc.vector.tensor_scalar(moments[:, par, 1:2], moments[:, par, 1:2], EPS, None, ALU.add)\
                  .then_inc(moments_ready, 1)

            def offset_of(tile, par):
                dve.wait_ge(rstd_ready, tile + 1)
                nc.vector.scalar_tensor_tensor(out=offset[:, par:par + 1], in0=moments[:, par, 0:1], scalar=-1.0,
                                               in1=rstd[:, par:par + 1], op0=ALU.mult, op1=ALU.mult)\
                  .then_inc(offset_ready, 1)

            nc.vector.memset(peaks[:, 7:8], 0.0).then_inc(peaks_ready, 1)
            per = TILES // X_LOADS * P
            for i in range(X_LOADS):
                dve.wait_ge(x_loaded[i], 16)
                nc.vector.tensor_reduce(peaks[:, i:i + 1], x_flat[:, i * per:(i + 1) * per], AX.X, ALU.max,
                                        apply_absolute_value=True).then_inc(peaks_ready, 1)
            dve.wait_ge(weights_loaded, 16 * 3)
            nc.vector.tensor_reduce(peaks[:, 4:7], w_in[:, :, :], AX.X, ALU.max, apply_absolute_value=True)\
              .then_inc(peaks_ready, 1)
            dve.wait_ge(peaks_shared, 1)
            nc.vector.tensor_reduce(x_peak[:, :], peaks_all[:, 0:X_LOADS], AX.X, ALU.max).then_inc(setup, 1)
            dve.wait_ge(setup, 1)
            nc.vector.tensor_scalar(bounds[:, :], peaks_all[:, 4:7], x_peak[:, :], float(D), ALU.mult, ALU.mult)\
              .then_inc(setup, 1)
            dve.wait_ge(setup, 2)
            nc.vector.tensor_scalar(recip2[:, :], bounds[:, :], 2.0 ** -60, None, ALU.max).then_inc(setup, 1)
            dve.wait_ge(setup, 3)
            nc.vector.tensor_scalar(pow2[:, :].bitcast(I32), recip2[:, :].bitcast(I32), 0x7F800000, None,
                                    ALU.bitwise_and).then_inc(setup, 1)
            dve.wait_ge(setup, 4)
            nc.vector.reciprocal(recip2[:, :], pow2[:, :]).then_inc(setup, 1)
            dve.wait_ge(setup, 5)
            nc.vector.tensor_scalar(factors[:, :], recip2[:, :], LIMIT, None, ALU.mult).then_inc(setup, 1)
            nc.vector.tensor_tensor(qk_pow2[:, :], pow2[:, 0:1], pow2[:, 1:2], ALU.mult).then_inc(setup, 1)
            dve.wait_ge(setup, 7)
            nc.vector.tensor_scalar(exp_scale[:, :], qk_pow2[:, :], SCALE / LIMIT ** 2, None, ALU.mult).then_inc(setup, 1)
            nc.vector.tensor_scalar(neg_scale[:, :], qk_pow2[:, :], -SCALE / LIMIT ** 2, None, ALU.mult)\
              .then_inc(setup, 1)
            nc.vector.tensor_scalar(v_back[:, :], pow2[:, 2:3], 1.0 / LIMIT, None, ALU.mult).then_inc(setup, 1)
            for kind, n in warm:
                if kind == "job":
                    what, h, c, chunks = jobs[n]
                    dve.wait_ge(hi_split, n + 1)
                    src = projection(n, chunks)
                    cols = slice(c * CHUNK, (c + chunks) * CHUNK)
                    if what == "v":
                        src = src.rearrange("p (a d) -> p a d", d=DH)
                        v = v_split[:, c * BLOCKS:(c + chunks) * BLOCKS, :, :, :].rearrange("p t h s d -> p (t h) s d")
                        hi, lo, factor = v[:, :, 0, :], v[:, :, 1, :], factors[:, 2:3]
                    elif what == "k":
                        hi, lo, factor = k_hi_stage[:, cols], k_lo_stage[:, cols], factors[:, 1:2]
                    elif what == "q":
                        src = src.rearrange("p (c k) -> p c k", k=CHUNK)
                        parts = q_stage[:, c:c + chunks, :, :]
                        hi, lo, factor = parts[:, :, 0, :], parts[:, :, 1, :], factors[:, 0:1]
                    else:
                        hi, lo, factor = q_hi[:, h, cols], q_lo[:, h, cols], factors[:, 0:1]
                    nc.vector.scalar_tensor_tensor(out=lo, in0=src, scalar=factor, in1=hi, op0=ALU.mult,
                                                   op1=ALU.subtract).then_inc(lo_split, 1)
                    for part in {2: (0, 1), 3: (2,), 4: (3,)}.get(n, ()):
                        dve.wait_ge(adj_loaded[0], 16)
                        c = slice(part * WIDTH, (part + 1) * WIDTH)
                        nc.vector.tensor_scalar(mask[:, 0, c], adj_in[:, 0, c], 0.0, MASKED, ALU.is_le, ALU.mult)\
                          .then_inc(masked, 1)
                else:
                    h, j = divmod(n, CH)
                    mask_max(n, h, 0, 0, j, n % 2, -1)
                    if n == CH:
                        top_of(0, 0)
            lower_part(0, 0)

            def pair(p, first, last):
                for s in range(PAIR_STEPS):
                    k, i = divmod(s, STEPS)
                    h, r = k % 2, k // 2
                    n, unit, tile = p * PAIR_STEPS + s, 4 * p + k, 2 * p + r
                    if not (last and k >= 2):
                        mask_max(STEP * n + AHEAD, h, tile + 1, 1 - r, STEP * i, 0, n)
                    if i == 0 and not (last and k == 3):
                        top_of(unit + 1, 1 - h)
                    if i == 0 and h == 1:
                        sum_up(unit, tile, r)
                    if not (last and s + 1 >= PAIR_STEPS):
                        lower_part(n + 1, s + 1)
                    if last and s + TURN_AHEAD in SHARED:
                        upper_part(n + TURN_AHEAD, s + TURN_AHEAD)
                    if i == 0 and h == 1:
                        invert_sums(tile, r)
                    if not (last and k >= 2):
                        mask_max(STEP * n + AHEAD + 1, h, tile + 1, 1 - r, STEP * i + 1, 1, n)
                    if h == 1 and i == 2 and not (first and r == 0):
                        leaky(tile - 1)
                    if not first:
                        if h == 0 and i == 1:
                            statistics(tile - 2, r)
                        if h == 0 and i == 2:
                            mean_variance(tile - 2, r)
                        if h == 0 and i == 3:
                            add_eps(tile - 2, r)
                        if h == 1 and i == 2:
                            offset_of(tile - 2, r)

            pair(0, True, False)
            with dve.Fori(1, PAIRS - 1) as p:
                pair(p, False, False)
            pair(PAIRS - 1, False, True)
            for t in (TILES - 2, TILES - 1):
                if t == TILES - 1:
                    leaky(t)
                statistics(t, t % 2)
                mean_variance(t, t % 2)
                add_eps(t, t % 2)
                offset_of(t, t % 2)

        @block.tensor
        def _(pe):
            def score(g, h, tile, j, slot):
                wait(pe, scores_taken, g - 1)
                tile_cols, c = bass.ds(tile * P, P), slice(j * CHUNK, (j + 1) * CHUNK)
                nc.tensor.matmul(ps[:, SCORE + slot, :], q_hi[:, h, tile_cols], k_split[:, h, c], start=True, stop=False)
                nc.tensor.matmul(ps[:, SCORE + slot, :], q_lo[:, h, tile_cols], k_split[:, h, c], start=False, stop=True)\
                  .then_inc(scored, 1)

            def turn(n, s, unit, h):
                i = s % STEPS
                pe.wait_ge(probs_ready, STEPS * unit + i + 1)
                wait(pe, lo_ready, n - 1)
                for b in range(STEP * BLOCKS):
                    c = slice(i * WIDTH + b * P, i * WIDTH + (b + 1) * P)
                    last = nc.tensor.transpose(turned_probs(s)[:, b * P:(b + 1) * P], rows[:, h, c], ident[:, :])
                last.then_inc(turned, 1)

            def attend(n, s, unit, tile, h, half):
                i = s % STEPS
                if half == 0:
                    pe.wait_ge(lo_ready, n + 1)
                if half == 0 and i == 0:
                    wait(pe, scaled, unit - 1)
                    if h == 1:
                        wait(pe, projection_ready, tile)
                for b in range(half * BLOCKS, (half + 1) * BLOCKS):
                    c = slice(b * P, (b + 1) * P)
                    v = v_split[:, i * STEP * BLOCKS + b, h, :, :].rearrange("p s d -> p (s d)")
                    nc.tensor.matmul(ps[:, SAT + h, 0:2 * DH], p_hi[:, s % 4, c], v,
                                     start=(i == 0 and b == 0), stop=False, skip_group_check=True)
                    last = nc.tensor.matmul(ps[:, SAT + h, 0:DH], p_lo[:, s % 4, c], v[:, 0:DH], start=False,
                                            stop=(i == STEPS - 1 and b == STEP * BLOCKS - 1), skip_group_check=True)
                if half == STEP - 1:
                    last.then_inc(attended, 1)

            def turn_sat(tile):
                pe.wait_ge(merged, tile + 1)
                nc.tensor.transpose(ps[:, SAT + 1, SIDE_T:SIDE_T + P], sat[:, :], ident[:, :]).then_inc(sat_turned, 1)

            def project_sat(tile):
                pe.wait_ge(sat_ready, tile + 1)
                w = w_out[:, :, :].rearrange("p s d -> p (s d)")[:, bass.ds(tile // (TILES // 2) * P, P)]
                nc.tensor.matmul(ps[:, SAT + 1, SIDE_P:SIDE_P + P], sat_cols[:, :], w, start=True, stop=True)\
                  .then_inc(sat_projected, 1)

            pe.wait_ge(ident_ready, 2)
            for n in range(CH):
                if n % 2 == 0:
                    pe.wait_ge(x_loaded[n // 2], 16)
                wait(pe, x_taken, n - WARM_BANKS + 1)
                for b in range(BLOCKS):
                    last = nc.tensor.transpose(ps[:, 2 + n % WARM_BANKS, b * P:(b + 1) * P],
                                               x_rows[:, n * BLOCKS + b, :], ident[:, :])
                last.then_inc(x_turned, 1)
            pe.wait_ge(weights_loaded, 16 * 3)
            pe.wait_ge(twice_loaded, 16 * 2)
            for kind, n in warm_pe:
                if kind == "score":
                    h, j = divmod(n, CH)
                    if j == 0:
                        pe.wait_ge(lo_split, early + 1 if h == 1 else 1)
                    if h == 0 and j % STEP == 0:
                        pe.wait_ge(k_placed[j // STEP], 16 * 2)
                    if h == 1 and j == 0:
                        pe.wait_ge(k_placed_second, 16 * 2)
                    score(n, h, 0, j, n % 2)
                    continue
                what, h, c, chunks = jobs[n]
                if n < WARM_BANKS // 2:
                    pe.wait_ge(x_taken, min(2 * n + CH - WARM_BANKS + STEP, CH))
                else:
                    pe.wait_ge(lo_split, n - WARM_BANKS // 2 + 1)
                target = projection(n, chunks)
                if what == "v":
                    for b in range(chunks * BLOCKS):
                        keys = slice(c * CHUNK + b * P, c * CHUNK + (b + 1) * P)
                        last = nc.tensor.matmul(target[:, b * P:(b + 1) * P], x_cols[:, keys], w_in[:, 2, :],
                                                start=True, stop=True)
                else:
                    if what == "q first":
                        w = w_q_twice[:, h, :, :].rearrange("p r d -> p (r d)")
                    else:
                        w = w_in[:, 0 if what == "q" else 1, :]
                    for b in range(chunks):
                        last = nc.tensor.matmul(target[:, b * CHUNK:(b + 1) * CHUNK], w,
                                                x_cols[:, (c + b) * CHUNK:(c + b + 1) * CHUNK], start=True, stop=True)
                last.then_inc(projected, 1)
            for n in range(TURN_AHEAD):
                pe.wait_ge(lo_split, max(m for m in range(len(jobs)) if bank_of(m) == TURN + STEP * n) + 1)
                turn(n, n, 0, 0)
            pe.wait_ge(lo_split, len(jobs))

            def pair(p, last):
                for s in range(PAIR_STEPS):
                    k, i = divmod(s, STEPS)
                    h, r = k % 2, k // 2
                    n, unit, tile = p * PAIR_STEPS + s, 4 * p + k, 2 * p + r
                    if not (last and k >= 2):
                        score(STEP * n + AHEAD, h, tile + 1, STEP * i, 0)
                    if not (last and s + TURN_AHEAD >= PAIR_STEPS):
                        ahead = s + TURN_AHEAD
                        turn(n + TURN_AHEAD, ahead, 4 * p + ahead // STEPS, ahead // STEPS % 2)
                    attend(n, s, unit, tile, h, 0)
                    if h == 0 and i == 2 and not (isinstance(p, int) and p == 0 and k == 0):
                        turn_sat(tile - 1)
                    if not (last and k >= 2):
                        score(STEP * n + AHEAD + 1, h, tile + 1, STEP * i + 1, 1)
                    attend(n, s, unit, tile, h, 1)
                    if h == 0 and i == 3 and not (isinstance(p, int) and p == 0 and k == 0):
                        project_sat(tile - 1)

            pe.wait_ge(w_out_ready, 1)
            pair(0, False)
            pe.wait_ge(q_placed, 16 * 4 * HEADS)
            with pe.Fori(1, PAIRS - 1) as p:
                pair(p, False)
            pair(PAIRS - 1, True)
            turn_sat(TILES - 1)
            project_sat(TILES - 1)


_INS = ["x", "adj", "L0_gnn_Wq", "L0_gnn_Wk", "L0_gnn_Wv", "L0_gnn_weightr", "L0_gnn_weightd", "L0_gnn_bias"]


def kernel(**inputs):
    import numpy as _np
    import concourse.bacc as _bacc
    from concourse import mybir as _mybir
    from concourse.bass_utils import run_bass_kernel_spmd as _run

    nc = _bacc.Bacc("TRN2", target_bir_lowering=False, num_devices=1)
    arrays, args = {}, []
    for name in _INS:
        a = _np.ascontiguousarray(inputs[name])
        arrays[f"in_{name}_dram"] = a
        args.append(nc.dram_tensor(f"in_{name}_dram", a.shape, _mybir.dt.from_np(a.dtype), kind="ExternalInput").ap())
    shape = inputs["x"].shape
    args.append(nc.dram_tensor("out_0_dram", shape, _mybir.dt.float32, kind="ExternalOutput").ap())
    gnn_layer(nc, *args)
    r = _run(nc, [arrays], core_ids=[0])
    return r.results[0]["out_0_dram"]
```
